# Optimizing a Trainium2 kernel written in Bass

```python
import numpy as np
import jax
import jax.numpy as jnp

def _softmax(x, axis=-1):
    return jax.nn.softmax(x, axis=axis)

def _gelu(x):
    return jax.nn.gelu(x, approximate=True)

def _silu(x):
    return jax.nn.silu(x)

def _sigmoid(x):
    return jax.nn.sigmoid(x)

def _layernorm(x, axis=-1, eps=1e-05):
    m = jnp.mean(x, axis=axis, keepdims=True)
    v = jnp.var(x, axis=axis, keepdims=True)
    return (x - m) / jnp.sqrt(v + eps)

def _scatter_add(tgt, idx, src, axis=0):
    return tgt.at[idx].add(src)

def _segment_sum(src, seg, n):
    return jax.ops.segment_sum(src, seg, n)
kernel_name = 'mk_adj_resnorm_d1_adj_r2_33b9d9'

def setup_inputs(seed: int=0):
    np.random.seed(seed)
    _w = jnp.asarray

    def _rec_inputs():
        import jax
        import jax.numpy as jnp
        _gk = jax.random.key(seed)
        x = -0.0001538 + 1 * jax.random.normal(jax.random.fold_in(_gk, 1), (16, 512, 384), jnp.float32)
        _a = jax.random.bernoulli(jax.random.fold_in(_gk, 2), 0.03125, (16, 512, 512))
        _a = jnp.logical_or(_a, jnp.swapaxes(_a, -1, -2))
        _a = jnp.logical_or(_a, jnp.eye(512, dtype=bool))
        _af = _a.astype(jnp.float32)
        _af = _af * jax.random.uniform(jax.random.fold_in(_gk, 3), (16, 512, 512), jnp.float32, 0.05, 4.42607)
        adj = _af
        return (x, adj)
    x, adj = _rec_inputs()

    def _L0_gnn_setup():
        import jax, jax.numpy as jnp
        import numpy as np
        NUM_HEADS = 12
        HIDDEN = 384
        HEAD = HIDDEN // NUM_HEADS
        SCALE = HIDDEN ** (-0.5)
        key = jax.random.key(seed)
        ks = jax.random.split(key, 8)
        B, N = (16, 256)
        std = HIDDEN ** (-0.5)
        return {'x': jax.random.normal(ks[0], (B, N, HIDDEN), dtype=jnp.float32), 'encoding_bias': jax.random.normal(ks[1], (B, N, N), dtype=jnp.float32), 'Wq': jax.random.normal(ks[2], (HIDDEN, HIDDEN), dtype=jnp.float32) * std, 'Wk': jax.random.normal(ks[3], (HIDDEN, HIDDEN), dtype=jnp.float32) * std, 'Wv': jax.random.normal(ks[4], (HIDDEN, HIDDEN), dtype=jnp.float32) * std, 'bv': jax.random.normal(ks[5], (HIDDEN,), dtype=jnp.float32) * 0.01, 'Wo': jax.random.normal(ks[6], (HIDDEN, HIDDEN), dtype=jnp.float32) * std, 'bo': jax.random.normal(ks[7], (HIDDEN,), dtype=jnp.float32) * 0.01}
    _L0_gnn_all = _L0_gnn_setup()
    _L0_gnn_in = {k: v for k, v in _L0_gnn_all.items() if k in ('Wq', 'Wk', 'Wv', 'bv', 'Wo', 'bo')}
    del _L0_gnn_all
    return {'x': x, 'adj': adj, 'L0_gnn_Wq': _L0_gnn_in['Wq'], 'L0_gnn_Wk': _L0_gnn_in['Wk'], 'L0_gnn_Wv': _L0_gnn_in['Wv'], 'L0_gnn_bv': _L0_gnn_in['bv'], 'L0_gnn_Wo': _L0_gnn_in['Wo'], 'L0_gnn_bo': _L0_gnn_in['bo']}

def reference(x, adj, L0_gnn_Wq, L0_gnn_Wk, L0_gnn_Wv, L0_gnn_bv, L0_gnn_Wo, L0_gnn_bo):
    import jax
    import jax.numpy as jnp

    def _L0_gnn_ref(x, encoding_bias, Wq, Wk, Wv, bv, Wo, bo):
        import jax, jax.numpy as jnp
        import numpy as np
        NUM_HEADS = 12
        HIDDEN = 384
        HEAD = HIDDEN // NUM_HEADS
        SCALE = HIDDEN ** (-0.5)
        B, N, _ = x.shape
        q = (x @ Wq.T).reshape(B, N, NUM_HEADS, HEAD)
        k = (x @ Wk.T).reshape(B, N, NUM_HEADS, HEAD)
        v = (x @ Wv.T + bv).reshape(B, N, NUM_HEADS, HEAD)
        a = jnp.einsum('bnhd,bmhd->bhnm', q, k) * SCALE + encoding_bias[:, None, :, :]
        pad_mask = jnp.all(a == 0, axis=-1)
        a = jnp.where(pad_mask[..., None], -jnp.inf, a)
        a = jax.nn.softmax(a, axis=-1)
        a = jnp.nan_to_num(a)
        o = jnp.einsum('bhnm,bmhd->bnhd', a, v).reshape(B, N, HIDDEN)
        return o @ Wo.T + bo
    x = _layernorm(x + _L0_gnn_ref(x, adj, L0_gnn_Wq, L0_gnn_Wk, L0_gnn_Wv, L0_gnn_bv, L0_gnn_Wo, L0_gnn_bo), axis=-1)
    return x

_drawn_inputs = setup_inputs


def setup_inputs(seed=0):
    import zlib

    import numpy as np

    out = dict(_drawn_inputs(seed))
    spreads = {}
    factors = {'L0_gnn_bv': 5.148, 'L0_gnn_bo': 5.682}
    for name, (base, spread) in spreads.items():
        noise = np.random.default_rng([zlib.crc32(name.encode()), seed]).standard_normal(out[name].shape)
        drawn = base * np.exp(spread * noise) if base else spread * noise
        out[name] = jnp.asarray(drawn.astype(out[name].dtype))
    for name, factor in factors.items():
        out[name] = (out[name] * factor).astype(out[name].dtype)
    return out
```

```python
from contextlib import ExitStack

import concourse.bass as bass
from concourse import mybir

F32 = mybir.dt.float32
F32R = mybir.dt.float32r
ALU = mybir.AluOpType
ACT = mybir.ActivationFunctionType
AX = mybir.AxisListType

B, N, D = 16, 512, 384
HEADS = 12
HD = D // HEADS
P = 128
SCALE = float(D) ** -0.5
EPS = 1e-5
BIG = 3.0e38

G = D // P
A = P // HD
NT = N // P
HALVES = 2
PER_HALF = NT // HALVES
UNITS = G * HALVES * A * PER_HALF
UNITS_G = UNITS // G
UNITS_H = UNITS_G // HALVES
NHALF = G * HALVES
HN = N // HALVES
BLOCKS = 3
STACK_DMAS = BLOCKS * 2 * A
SLOTS = 3

SCORES_AHEAD = 3
AHEAD = 2

CHUNKS = [
    (3, "r", 2, -1), (3, "v", 0, 0), (4, "v", 1, 0), (5, "v", 2, 0), (6, "v", 3, 0),
    (8, "o", 0, -1), (10, "o", 1, -1), (11, "o", 2, -1), (12, "o", 3, -1),
    (13, "x", 0, 1), (14, "x", 1, 1), (15, "x", 2, 1),
    (18, "k", 0, 1), (19, "r", 0, 0), (20, "q", 0, 1), (22, "lin", 0, 1),
    (23, "k", 1, 1), (26, "q", 1, 1), (28, "lin", 1, 1),
    (34, "k", 2, 1), (35, "r", 1, 0), (37, "q", 2, 1), (39, "lin", 2, 1),
]
VECTOR_READS_AFTER = 1
BANKS = 3
FIRST_CHUNKS = [("w", i) for i in range(4 * G)] + [("x", t) for t in range(G)] + [
    (kind, g) for g in range(G) for kind in ("k", "q", "lin")]
LAST_CHUNKS = [("r", 2)] + [("o", t) for t in range(NT)]
PV_STEP = {8 * h + 9: (h, 0) for h in range(NHALF - 1)} | {1: (NHALF - 1, -1)}
ADJ_SUM_STEP = [4, 8]
VECTOR_UNITS = [u for u in range(UNITS) if u % 3 == 1]


def present(rel, first, last):
    return not (first and rel < 0) and not (last and rel > 0)


def unit(u):
    g, r = divmod(u, UNITS_G)
    half, r = divmod(r, UNITS_H)
    a, n2 = divmod(r, PER_HALF)
    return g, half, a, n2, half * PER_HALF + n2


def chunk_bank(i):
    return i % BANKS


def before_in_bank(i, b, first, last):
    for j in range(i - 1, -1, -1):
        if chunk_bank(j) == chunk_bank(i) and present(CHUNKS[j][3], first, last):
            return CHUNKS[j][1], CHUNKS[j][2], b + CHUNKS[j][3]
    if first:
        return before_in_list(FIRST_CHUNKS, len(FIRST_CHUNKS), i, 0)
    for j in range(len(CHUNKS) - 1, -1, -1):
        if chunk_bank(j) == chunk_bank(i):
            return CHUNKS[j][1], CHUNKS[j][2], b - 1 + CHUNKS[j][3]


def before_in_list(chunks, upto, i, b):
    for j in range(upto - 1, -1, -1):
        if chunk_bank(j) == chunk_bank(i):
            return *chunks[j], b
    return None


def wait(engine, semaphore, count):
    if not (isinstance(count, int) and count <= 0):
        engine.wait_ge(semaphore, count)


def wait_apart(engine, semaphore, count, carried, met):
    count = worked_out(engine, count)
    engine.wait_ge(carried, met)
    engine.wait_ge(semaphore, count)


def worked_out(engine, count):
    return count if isinstance(count, int) else engine.to_reg(count)


def vector_evacs(b, u):
    return b * len(VECTOR_UNITS) + sum(v <= u for v in VECTOR_UNITS) - (
        sum(v > UNITS + u for v in VECTOR_UNITS) if u < 0 else 0)


def scalar_evacs(b, u):
    scalar_units = [v for v in range(UNITS) if v not in VECTOR_UNITS]
    return b * len(scalar_units) + sum(v <= u for v in scalar_units) - (
        sum(v > UNITS + u for v in scalar_units) if u < 0 else 0)


def build(nc, x, adj, wq, wk, wv, bv, wo, bo, out):
    with ExitStack() as ctx:
        def sb(name, shape, dt=F32):
            return ctx.enter_context(nc.sbuf_tensor(name, shape, dt))

        def bank(name):
            return ctx.enter_context(nc.psum_tensor(name, [P, N], F32))

        def sem(name):
            return ctx.enter_context(nc.semaphore(name))

        ident = sb("ident", [P, P])
        head_mask = sb("head_mask", [P, P])
        bv_rows, bo_rows = sb("bv_rows", [P, D]), sb("bo_rows", [P, D])
        w_hi, w_lo = sb("w_hi", [P, 4, G, D], F32R), sb("w_lo", [P, 4, G, D], F32R)
        x_rows = sb("x_rows", [P, NT, D])
        resid = sb("resid", [P, NT, D])
        xt_hi, xt_lo = sb("xt_hi", [P, G, N], F32R), sb("xt_lo", [P, G, N], F32R)
        kt_hi, kt_lo = sb("kt_hi", [P, 2, N], F32R), sb("kt_lo", [P, 2, N], F32R)
        qt_hi, qt_lo = sb("qt_hi", [P, 2, N], F32R), sb("qt_lo", [P, 2, N], F32R)
        k_stack = sb("k_stack", [BLOCKS * HD, G, A, N], F32R)
        q_stack = sb("q_stack", [BLOCKS * HD, G, A, N], F32R)
        adj_rows = sb("adj_rows", [P, NT, N])
        v_rows = sb("v_rows", [P, NT, D])
        neg_a = sb("neg_a", [P, SLOTS, N])
        p_rows = sb("p_rows", [P, SLOTS, N])
        pt = sb("pt", [P, 2, A * NT * HN])
        o_cols = sb("o_cols", [P, N])
        ot_hi, ot_lo = sb("ot_hi", [P, G, N], F32R), sb("ot_lo", [P, G, N], F32R)
        y = sb("y", [P, 2, D])
        neg_max, row_sum = sb("neg_max", [P, UNITS]), sb("row_sum", [P, UNITS])
        k_sum = sb("k_sum", [P, G])
        k_sum_heads = sb("k_sum_heads", [P, P], F32R)
        lin_next, lin = sb("lin_next", [P, UNITS]), sb("lin", [P, UNITS])
        adj_sum = sb("adj_sum", [P, NT])
        a_sum = sb("a_sum", [P, UNITS_G])
        max_zero, live = sb("max_zero", [P, UNITS_G]), sb("live", [P, UNITS_G])
        recip, recip_live = sb("recip", [P, UNITS_G]), sb("recip_live", [P, UNITS_G])
        recip_heads = sb("recip_heads", [P, UNITS_G, HD])
        bn, mv, variance = sb("bn", [P, 2, 6]), sb("mv", [P, 2, 2]), sb("variance", [P, 2, 1])
        neg_mean, rstd, minus_half = sb("neg_mean", [P, 2, 1]), sb("rstd", [P, 2, 1]), sb("minus_half", [P, 1])

        score_bank = [bank(f"score_bank{i}") for i in range(2)]
        turn_bank = [bank(f"turn_bank{i}") for i in range(2)]
        o_bank = bank("o_bank")
        chunk_banks = [bank(f"chunk_bank{i}") for i in range(BANKS)]

        w_loaded, bias_loaded, x_loaded, resid_loaded = map(sem, ("w_loaded", "bias_loaded", "x_loaded", "resid_loaded"))
        adj_loaded = [sem(f"adj_loaded{t}") for t in range(NT)]
        stack_loaded = [sem(f"stack_loaded{g}") for g in range(G)]
        stored = [sem(f"stored{i}") for i in range(2)]
        ident_ready, mask_cleared, mask_ready = sem("ident_ready"), sem("mask_cleared"), sem("mask_ready")
        w_turned, w_hi_ready, w_lo_ready = sem("w_turned"), sem("w_hi_ready"), sem("w_lo_ready")
        x_turned, x_hi_ready, x_lo_ready = sem("x_turned"), sem("x_hi_ready"), sem("x_lo_ready")
        kq_done, kq_hi_ready, kq_lo_ready = sem("kq_done"), sem("kq_hi_ready"), sem("kq_lo_ready")
        k_sum_ready, lin_done, lin_read = sem("k_sum_ready"), sem("lin_done"), sem("lin_read")
        v_done, v_ready = sem("v_done"), sem("v_ready")
        scores_done, max_done, exp_done = sem("scores_done"), sem("max_done"), sem("exp_done")
        turned, pt_by_vector, pt_by_scalar = sem("turned"), sem("pt_by_vector"), sem("pt_by_scalar")
        pv_done, adj_summed, lin_moved, stats = sem("pv_done"), sem("adj_summed"), sem("lin_moved"), sem("stats")
        recip_ready, r_done, r_ready = sem("recip_ready"), sem("r_done"), sem("r_ready")
        o_ready, o_hi_ready, o_lo_ready = sem("o_ready"), sem("o_hi_ready"), sem("o_lo_ready")
        norm_scalars = sem("norm_scalars")
        proj_done, norm_step, y_ready, resid_ready = sem("proj_done"), sem("norm_step"), sem("y_ready"), sem("resid_ready")

        def pt_tile(h):
            return pt[:, h % 2, :].rearrange("p (a m n) -> p a m n", a=A, m=NT)

        w_rows = pt[:, :, :].rearrange("p b f -> p (b f)")[:, 0:4 * G * D].rearrange("p (w t i) -> p w t i", w=4, t=G)

        def body_chunks(step, first, last):
            for i, (at, kind, index, rel) in enumerate(CHUNKS):
                if at == step and present(rel, first, last):
                    yield i, kind, index, rel

        def ahead(step, lead, last):
            u = step + lead
            if u < UNITS:
                return u, 0
            return (None, 0) if last else (u - UNITS, 1)

        block = ctx.enter_context(nc.Block())

        def bodies(engine, body, last_part):
            body(0, True, False)
            with engine.Fori(1, B - 1) as b:
                body(b, False, False)
            body(B - 1, False, True)
            last_part()

        @block.sync
        def _(sp):
            def load_x(b):
                wait(sp, x_turned, G * b)
                sp.dma_start(x_rows[:, :, :], x[bass.ds(b, 1)].rearrange("o (t p) d -> p (o t) d", p=P)).then_inc(x_loaded, 16)

            def load_adj(b, t):
                sp.dma_start(adj_rows[:, t, :], adj[bass.ds(b, 1), t * P:(t + 1) * P, :].rearrange("o p n -> p (o n)")).then_inc(adj_loaded[t], 16)

            def load_resid(b):
                stores = worked_out(sp, 16 * (NT // 2) * b)
                wait(sp, norm_step, 4 * NT * b)
                for slot in stored:
                    wait(sp, slot, stores)
                sp.dma_start(resid[:, :, :], x[bass.ds(b, 1)].rearrange("o (t p) d -> p (o t) d", p=P)).then_inc(resid_loaded, 16)

            def stack(b, g):
                parts_made = worked_out(sp, 2 * G * b + 2 * g + 2)
                wait(sp, scores_done, UNITS * (b - 1) + UNITS_G * (g + 1))
                sp.wait_ge(kq_lo_ready, parts_made)
                for a in range(A):
                    own = slice(HD * a, HD * a + HD)
                    for to, parts in ((k_stack, (kt_hi, kt_lo, kt_hi)), (q_stack, (qt_hi, qt_hi, qt_lo))):
                        for j, part in enumerate(parts):
                            sp.dma_start(to[HD * j:HD * j + HD, g, a, :].bitcast(F32), part[own, g % 2, :].bitcast(F32)).then_inc(stack_loaded[g], 16)

            def store(b, t):
                sp.wait_ge(y_ready, NT * b + t + 1)
                sp.dma_start(out[bass.ds(b, 1), t * P:(t + 1) * P, :].rearrange("o p d -> p (o d)"), y[:, t % 2, :]).then_inc(stored[t % 2], 16)

            for w, src in enumerate((wq, wk, wv, wo)):
                sp.dma_start(w_rows[:, w, :, :], src.rearrange("(t p) i -> p t i", p=P)).then_inc(w_loaded, 16)
            load_x(0)
            for rows, src in ((bv_rows, bv), (bo_rows, bo)):
                sp.dma_start(rows[:, :], src.rearrange("(o d) -> o d", o=1).broadcast_to([P, D])).then_inc(bias_loaded, 16)
            for t in range(NT):
                load_adj(0, t)
            for g in range(G):
                stack(0, g)

            def body(b, first, last):
                if not last:
                    load_x(b + 1)
                if not first:
                    for t in range(NT):
                        store(b - 1, t)
                load_resid(b)
                if not last:
                    stack(b + 1, 0)
                    stack(b + 1, 1)
                    for half in range(HALVES):
                        sp.wait_ge(max_done, UNITS * b + UNITS - UNITS_H * (HALVES - 1 - half))
                        for n2 in range(PER_HALF):
                            load_adj(b + 1, half * PER_HALF + n2)
                    stack(b + 1, 2)

            def last_part():
                for t in range(NT):
                    store(B - 1, t)
                for slot in stored:
                    sp.wait_ge(slot, 16 * NT // 2 * B)

            bodies(sp, body, last_part)

        @block.gpsimd
        def _(pool):
            nc.gpsimd.memset(ident[:, :], 0.0).then_inc(mask_cleared, 1)
            nc.gpsimd.memset(head_mask[:, :], 0.0).then_inc(mask_cleared, 1)
            nc.gpsimd.memset(minus_half[:, :], -0.5).then_inc(mask_cleared, 1)
            pool.wait_ge(mask_cleared, 3)
            nc.gpsimd.affine_select(out=ident[:, :], in_=ident[:, :], compare_op=ALU.not_equal, fill=1.0, base=0,
                                    pattern=[[-1, P]], channel_multiplier=1).then_inc(ident_ready, 1)
            pool.wait_ge(ident_ready, 1)
            for a in range(A):
                own = slice(HD * a, HD * a + HD)
                if a:
                    pool.wait_ge(mask_ready, a)
                nc.gpsimd.memset(head_mask[own, own], 1.0).then_inc(mask_ready, 1)

            def add_bias(b):
                pool.wait_ge(resid_loaded, 16 * (b + 1))
                nc.gpsimd.tensor_tensor(resid[:, :, :], resid[:, :, :], bo_rows[:, :].unsqueeze(1).broadcast_to([P, NT, D]),
                                        ALU.add).then_inc(resid_ready, 1)

            def spread(b, g):
                wait(pool, r_done, G * b + g)
                wait_apart(pool, stats, 6 * (G * b + g + 1), bias_loaded, 32)
                nc.gpsimd.tensor_copy(recip_heads[:, :, :], recip_live[:, :].unsqueeze(2).broadcast_to([P, UNITS_G, HD])).then_inc(recip_ready, 1)

            def low_part(b, g):
                pool.wait_ge(o_hi_ready, G * b + g + 1)
                nc.gpsimd.tensor_tensor(ot_lo[:, g, :], o_cols[:, :], ot_hi[:, g, :].bitcast(F32), ALU.subtract).then_inc(o_lo_ready, 1)

            def normalise(b, t):
                slot = t % 2
                wait_apart(pool, norm_step, 4 * (NT * b + t + 1), bias_loaded, 32)
                nc.gpsimd.tensor_scalar(neg_mean[:, slot, :], mv[:, slot, 0:1], -1.0, 0.0, ALU.mult, ALU.add).then_inc(norm_scalars, 1)
                nc.gpsimd.tensor_tensor(rstd[:, slot, :], variance[:, slot, :], minus_half[:, :], ALU.pow).then_inc(norm_scalars, 1)
                wait_apart(pool, norm_scalars, 2 * (NT * b + t + 1), bias_loaded, 32)
                nc.gpsimd.tensor_scalar(y[:, slot, :], y[:, slot, :], neg_mean[:, slot, :], rstd[:, slot, :], ALU.add, ALU.mult).then_inc(y_ready, 1)

            pool.wait_ge(mask_ready, A)
            pool.wait_ge(bias_loaded, 32)

            def body(b, first, last):
                if not first:
                    spread(b - 1, 2)
                    low_part(b - 1, 2)
                    for t in range(NT):
                        normalise(b - 1, t)
                add_bias(b)
                for g in range(G - 1):
                    spread(b, g)
                    low_part(b, g)

            def last_part():
                spread(B - 1, 2)
                low_part(B - 1, 2)
                for t in range(NT):
                    normalise(B - 1, t)

            bodies(pool, body, last_part)

        @block.tensor
        def _(pe):
            def turn_w(i, bank):
                w, t = divmod(i, G)
                for s in range(G):
                    last = pe.transpose(bank[:, s * P:(s + 1) * P], w_rows[:, w, s, t * P:(t + 1) * P], ident[:, :])
                last.then_inc(w_turned, 1)

            def turn_x(b, t, bank):
                pe.wait_ge(x_loaded, 16 * (b + 1))
                for s in range(NT):
                    last = pe.transpose(bank[:, s * P:(s + 1) * P], x_rows[:, s, t * P:(t + 1) * P], ident[:, :])
                last.then_inc(x_turned, 1)

            def three_products(dst, pairs, done):
                for n, (lhs, rhs) in enumerate(pairs):
                    last = pe.matmul(dst, lhs, rhs, start=(n == 0), stop=(n == len(pairs) - 1))
                last.then_inc(done, 1)

            def parts(left, left_cols, right, right_cols):
                return [(left[i][:, t, left_cols], right[j][:, t, right_cols])
                        for t in range(G) for i, j in ((0, 0), (0, 1), (1, 0))]

            def weight(w):
                return (w_hi[:, w], w_lo[:, w])

            def project_kq(b, w, g, bank):
                pe.wait_ge(x_lo_ready, G * (b + 1))
                three_products(bank[:, :], parts(weight(w), slice(g * P, (g + 1) * P), (xt_hi, xt_lo), slice(0, N)), kq_done)

            def linear_sums(b, g, bank):
                pe.wait_ge(k_sum_ready, G * b + g + 1)
                pe.wait_ge(kq_lo_ready, 2 * G * b + 2 * g + 2)
                for t in range(NT):
                    rows = slice(t * P, (t + 1) * P)
                    for n, part in enumerate((qt_hi, qt_lo)):
                        last = pe.matmul(bank[:, rows], part[:, g % 2, rows], k_sum_heads[:, :], start=(n == 0), stop=(n == 1))
                last.then_inc(lin_done, 1)

            def project_v(b, t, bank):
                three_products(bank[:, 0:D], parts((xt_hi, xt_lo), slice(t * P, (t + 1) * P), weight(2), slice(0, D)), v_done)

            def project_out(b, t, bank):
                pe.wait_ge(o_lo_ready, G * (b + 1))
                three_products(bank[:, 0:D], parts((ot_hi, ot_lo), slice(t * P, (t + 1) * P), weight(3), slice(0, D)), proj_done)

            def turn_recip(b, g, bank):
                pe.wait_ge(recip_ready, G * b + g + 1)
                for t in range(NT):
                    last = pe.transpose(bank[:, t * P:(t + 1) * P], recip_heads[:, t * A:(t + 1) * A, :].rearrange("p a d -> p (a d)"), ident[:, :])
                last.then_inc(r_done, 1)

            def scores(b, u):
                g, half, a, n2, t = unit(u)
                if u % UNITS_G == 0:
                    pe.wait_ge(stack_loaded[g], 16 * STACK_DMAS * (b + 1))
                wait(pe, max_done, UNITS * b + u - 1)
                pe.matmul(score_bank[u % 2][:, :], q_stack[:, g, a, t * P:(t + 1) * P], k_stack[:, g, a, :],
                          start=True, stop=True).then_inc(scores_done, 1)

            def turn_p(b, u):
                pe.wait_ge(exp_done, UNITS * b + u + 1)
                if (u - 2) % UNITS in VECTOR_UNITS:
                    wait(pe, pt_by_vector, vector_evacs(b, u - 2))
                else:
                    wait(pe, pt_by_scalar, scalar_evacs(b, u - 2))
                for m in range(NT):
                    last = pe.transpose(turn_bank[u % 2][:, m * P:(m + 1) * P], p_rows[:, u % SLOTS, m * P:(m + 1) * P], ident[:, :])
                last.then_inc(turned, 1)

            def weigh_v(b, h):
                g, half = divmod(h, HALVES)
                if half == 0:
                    wait(pe, o_ready, G * b + g)
                if h == 0:
                    pe.wait_ge(v_ready, NT * (b + 1))
                pe.wait_ge(pt_by_vector, vector_evacs(b, UNITS_H * (h + 1) - 1))
                pe.wait_ge(pt_by_scalar, scalar_evacs(b, UNITS_H * (h + 1) - 1))
                tile = pt_tile(h)
                for m in range(NT):
                    for a in range(A):
                        head = g * P + a * HD
                        last = pe.matmul(o_bank[a * HD:(a + 1) * HD, half * HN:(half + 1) * HN], v_rows[:, m, head:head + HD],
                                         tile[:, a, m, :], start=(m == 0), stop=(m == NT - 1), tile_position=(0, a * HD))
                last.then_inc(pv_done, 1)

            def chunk(b, kind, index, bank):
                if kind == "w":
                    turn_w(index, bank)
                if kind == "x":
                    turn_x(b, index, bank)
                if kind in ("k", "q"):
                    project_kq(b, int(kind == "k"), index, bank)
                if kind == "lin":
                    linear_sums(b, index, bank)
                if kind == "v":
                    project_v(b, index, bank)
                if kind == "o":
                    project_out(b, index, bank)
                if kind == "r":
                    turn_recip(b, index, bank)

            def bank_free(chunk):
                if chunk is not None:
                    kind, index, b = chunk
                    pe.wait_ge(*{
                        "w": (w_lo_ready, index + 1),
                        "x": (x_lo_ready, G * b + index + 1),
                        "k": (kq_lo_ready, 2 * G * b + 2 * index + 1),
                        "q": (kq_lo_ready, 2 * G * b + 2 * index + 2),
                        "lin": (lin_read, G * b + index + 1),
                        "v": (v_ready, NT * b + index + 1),
                        "o": (norm_step, 4 * (NT * b + index) + 1),
                        "r": (r_ready, G * b + index + 1),
                    }[kind])

            pe.wait_ge(ident_ready, 1)
            pe.wait_ge(w_loaded, 64)
            for i, (kind, index) in enumerate(FIRST_CHUNKS):
                bank_free(before_in_list(FIRST_CHUNKS, i, i, 0))
                if kind == "k" and index == 0:
                    pe.wait_ge(w_lo_ready, 4 * G)
                chunk(0, kind, index, chunk_banks[chunk_bank(i)])
            for u in range(SCORES_AHEAD):
                scores(0, u)

            def body(b, first, last):
                for s in range(UNITS):
                    u, rel = ahead(s, SCORES_AHEAD, last)
                    if u is not None:
                        scores(b + rel, u)
                    if s in PV_STEP and present(PV_STEP[s][1], first, last):
                        weigh_v(b + PV_STEP[s][1], PV_STEP[s][0])
                    turn_p(b, s)
                    for i, kind, index, rel in body_chunks(s, first, last):
                        bank_free(before_in_bank(i, b, first, last))
                        chunk(b + rel, kind, index, chunk_banks[chunk_bank(i)])

            def last_part():
                weigh_v(B - 1, NHALF - 1)
                for i, (kind, index) in enumerate(LAST_CHUNKS):
                    bank_free(before_in_list(LAST_CHUNKS, i, i, B - 1) or before_in_bank(len(CHUNKS) + (i - len(CHUNKS)) % BANKS, B - 1, False, True))
                    chunk(B - 1, kind, index, chunk_banks[chunk_bank(i)])

            bodies(pe, body, last_part)

        @block.scalar
        def _(act):
            def exponential(b, u):
                act.wait_ge(max_done, UNITS * b + u + 1)
                wait(act, turned, UNITS * b + u + 1 - SLOTS)
                nc.scalar.activation(p_rows[:, u % SLOTS, :], neg_a[:, u % SLOTS, :], ACT.Exp, bias=neg_max[:, u:u + 1],
                                     scale=-1.0, accum_out=row_sum[:, u:u + 1]).then_inc(exp_done, 1)

            def chunk(b, kind, index, bank, i):
                if kind == "w":
                    w, t = divmod(index, G)
                    act.wait_ge(w_turned, index + 1)
                    nc.scalar.activation(w_hi[:, w, t, :], bank[:, 0:D], ACT.Copy, scale=SCALE if w == 0 else 1.0).then_inc(w_hi_ready, 1)
                if kind == "x":
                    act.wait_ge(x_turned, G * b + index + 1)
                    nc.scalar.activation(xt_hi[:, index, :], bank[:, :], ACT.Copy).then_inc(x_hi_ready, 1)
                if kind in ("k", "q"):
                    act.wait_ge(kq_done, 2 * G * b + 2 * index + 1 + (kind == "q"))
                    if kind == "k":
                        wait(act, stack_loaded[{0: 2, 1: 1, 2: 0}[index]], 16 * STACK_DMAS * (b + (index == 2)))
                        nc.scalar.activation(kt_hi[:, index % 2, :], bank[:, :], ACT.Copy, accum_out=k_sum[:, index:index + 1]).then_inc(kq_hi_ready, 1)
                    else:
                        nc.scalar.activation(qt_hi[:, index % 2, :], bank[:, :], ACT.Copy).then_inc(kq_hi_ready, 1)
                if kind == "r":
                    act.wait_ge(r_done, G * b + index + 1)
                    wait(act, o_lo_ready, G * b + index)
                    nc.scalar.activation(o_cols[:, :], bank[:, :], ACT.Copy).then_inc(r_ready, 1)

            def round_o(b, g):
                act.wait_ge(o_ready, G * b + g + 1)
                if g == 0:
                    wait(act, proj_done, NT * b)
                nc.scalar.activation(ot_hi[:, g, :], o_cols[:, :], ACT.Copy).then_inc(o_hi_ready, 1)

            def take_pt(b, u):
                g, half, a, n2, t = unit(u)
                h = g * HALVES + half
                act.wait_ge(turned, UNITS * b + u + 1)
                wait(act, pv_done, NHALF * b + h - 1)
                nc.scalar.activation(pt_tile(h)[:, a, :, n2 * P:(n2 + 1) * P],
                                     turn_bank[u % 2][:, :].rearrange("p (m n) -> p m n", m=NT), ACT.Copy).then_inc(pt_by_scalar, 1)

            for i, (kind, index) in enumerate(FIRST_CHUNKS):
                chunk(0, kind, index, chunk_banks[chunk_bank(i)], i)
            for u in range(AHEAD):
                exponential(0, u)

            def body(b, first, last):
                for s in range(UNITS):
                    u, rel = ahead(s, AHEAD, last)
                    if u is not None:
                        exponential(b + rel, u)
                    if s not in VECTOR_UNITS:
                        take_pt(b, s)
                    for i, kind, index, rel in body_chunks(s, first, last):
                        chunk(b + rel, kind, index, chunk_banks[chunk_bank(i)], i)
                    for i, kind, index, rel in body_chunks(s - VECTOR_READS_AFTER - 2, first, last):
                        if kind == "r":
                            round_o(b + rel, index)

            def last_part():
                chunk(B - 1, "r", 2, chunk_banks[0], 0)
                round_o(B - 1, 2)

            bodies(act, body, last_part)

        @block.vector
        def _(dve):
            def row_max(b, u):
                g, half, a, n2, t = unit(u)
                if u in (0, 1, UNITS_H, UNITS_H + 1):
                    dve.wait_ge(adj_loaded[t], 16 * (b + 1))
                wait(dve, exp_done, UNITS * b + u + 1 - SLOTS)
                wait_apart(dve, scores_done, UNITS * b + u + 1, adj_loaded[t], 16)
                nc.vector.tensor_tensor_reduce(neg_a[:, u % SLOTS, :], score_bank[u % 2][:, :], adj_rows[:, t, :], -1.0, BIG,
                                               ALU.add, ALU.min, neg_max[:, u:u + 1]).then_inc(max_done, 1)

            def chunk(b, kind, index, bank):
                if kind == "w":
                    w, t = divmod(index, G)
                    dve.wait_ge(w_hi_ready, index + 1)
                    nc.vector.scalar_tensor_tensor(w_lo[:, w, t, :], bank[:, 0:D], SCALE if w == 0 else 1.0,
                                                   w_hi[:, w, t, :].bitcast(F32), ALU.mult, ALU.subtract).then_inc(w_lo_ready, 1)
                if kind == "x":
                    dve.wait_ge(x_hi_ready, G * b + index + 1)
                    nc.vector.tensor_tensor(xt_lo[:, index, :], bank[:, :], xt_hi[:, index, :].bitcast(F32), ALU.subtract).then_inc(x_lo_ready, 1)
                if kind in ("k", "q"):
                    hi, lo = (kt_hi, kt_lo) if kind == "k" else (qt_hi, qt_lo)
                    dve.wait_ge(kq_hi_ready, 2 * G * b + 2 * index + 1 + (kind == "q"))
                    if kind == "k":
                        nc.vector.tensor_scalar(k_sum_heads[:, :], head_mask[:, :], k_sum[:, index:index + 1], None, ALU.mult).then_inc(k_sum_ready, 1)
                    nc.vector.tensor_tensor(lo[:, index % 2, :], bank[:, :], hi[:, index % 2, :].bitcast(F32), ALU.subtract).then_inc(kq_lo_ready, 1)
                if kind == "lin":
                    dve.wait_ge(lin_done, G * b + index + 1)
                    of_heads = bank[:, :].rearrange("p (h n a d) -> p h a n d", h=HALVES, n=PER_HALF, a=A)[:, :, :, :, 0]
                    nc.vector.tensor_copy(lin_next[:, index * UNITS_G:(index + 1) * UNITS_G].rearrange("p (h a n) -> p h a n", h=HALVES, a=A),
                                          of_heads).then_inc(lin_read, 1)
                if kind == "v":
                    dve.wait_ge(v_done, NT * b + index + 1)
                    nc.vector.tensor_tensor(v_rows[:, index, :], bank[:, 0:D], bv_rows[:, :], ALU.add).then_inc(v_ready, 1)
                if kind == "o":
                    residual_norm(b, index, bank)

            def residual_norm(b, t, bank):
                done = 4 * (NT * b + t)
                slot = t % 2
                dve.wait_ge(proj_done, NT * b + t + 1)
                dve.wait_ge(resid_ready, b + 1)
                if t >= 2:
                    dve.wait_ge(stored[slot], 16 * (NT // 2 * b + t // 2))
                nc.vector.tensor_tensor(y[:, slot, :], bank[:, 0:D], resid[:, t, :], ALU.add).then_inc(norm_step, 1)
                dve.wait_ge(norm_step, done + 1)
                nc.vector.bn_stats(bn[:, slot, :], y[:, slot, :]).then_inc(norm_step, 1)
                wait_apart(dve, norm_step, done + 2, norm_step, 1)
                nc.vector.bn_aggr(mv[:, slot, :], bn[:, slot, :]).then_inc(norm_step, 1)
                dve.wait_ge(norm_step, done + 3)
                nc.vector.tensor_scalar(variance[:, slot, :], mv[:, slot, 1:2], EPS, None, ALU.add).then_inc(norm_step, 1)

            def sum_adj(b, half):
                nc.vector.tensor_reduce(adj_sum[:, half * PER_HALF:(half + 1) * PER_HALF],
                                        adj_rows[:, half * PER_HALF:(half + 1) * PER_HALF, :], AX.X, ALU.add).then_inc(adj_summed, 1)

            def move_lin(b):
                dve.wait_ge(lin_read, G * (b + 1))
                nc.vector.tensor_copy(lin[:, :], lin_next[:, :]).then_inc(lin_moved, 1)

            def reciprocals(b, g):
                cols = slice(g * UNITS_G, (g + 1) * UNITS_G)
                done = 6 * (G * b + g)

                def heads(ap):
                    return ap.rearrange("p (h a n) -> p h a n", h=HALVES, a=A)

                dve.wait_ge(exp_done, UNITS * b + (g + 1) * UNITS_G)
                dve.wait_ge(lin_moved, b + 1)
                dve.wait_ge(adj_summed, HALVES * (b + 1))
                nc.vector.tensor_tensor(heads(a_sum[:, :]), heads(lin[:, cols]),
                                        adj_sum[:, :].rearrange("p (h n) -> p h n", h=HALVES).unsqueeze(2).broadcast_to([P, HALVES, A, PER_HALF]),
                                        ALU.add).then_inc(stats, 1)
                nc.vector.tensor_scalar(max_zero[:, :], neg_max[:, cols], 0.0, None, ALU.is_equal).then_inc(stats, 1)
                nc.vector.reciprocal(recip[:, :], row_sum[:, cols]).then_inc(stats, 1)
                dve.wait_ge(stats, done + 2)
                nc.vector.scalar_tensor_tensor(live[:, :], a_sum[:, :], 0.0, max_zero[:, :], ALU.is_equal, ALU.mult).then_inc(stats, 1)
                dve.wait_ge(stats, done + 4)
                nc.vector.tensor_scalar(live[:, :], live[:, :], -1.0, 1.0, ALU.mult, ALU.add).then_inc(stats, 1)
                dve.wait_ge(stats, done + 5)
                wait(dve, recip_ready, G * b + g)
                nc.vector.tensor_tensor(recip_live[:, :].rearrange("p (h n a) -> p h a n", h=HALVES, a=A), heads(recip[:, :]),
                                        heads(live[:, :]), ALU.mult).then_inc(stats, 1)

            def divide_o(b, g):
                dve.wait_ge(r_ready, G * b + g + 1)
                dve.wait_ge(pv_done, NHALF * b + (g + 1) * HALVES)
                nc.vector.tensor_tensor(o_cols[:, :], o_bank[:, :], o_cols[:, :], ALU.mult).then_inc(o_ready, 1)

            def take_pt(b, u):
                g, half, a, n2, t = unit(u)
                h = g * HALVES + half
                dve.wait_ge(turned, UNITS * b + u + 1)
                wait(dve, pv_done, NHALF * b + h - 1)
                nc.vector.tensor_copy(pt_tile(h)[:, a, :, n2 * P:(n2 + 1) * P],
                                      turn_bank[u % 2][:, :].rearrange("p (m n) -> p m n", m=NT)).then_inc(pt_by_vector, 1)

            dve.wait_ge(mask_ready, A)
            dve.wait_ge(bias_loaded, 32)
            for i, (kind, index) in enumerate(FIRST_CHUNKS):
                chunk(0, kind, index, chunk_banks[chunk_bank(i)])
            for u in range(AHEAD):
                row_max(0, u)

            def body(b, first, last):
                for s in range(UNITS):
                    u, rel = ahead(s, AHEAD, last)
                    if u is not None:
                        row_max(b + rel, u)
                    if s == 0:
                        move_lin(b)
                    if s in ADJ_SUM_STEP:
                        sum_adj(b, ADJ_SUM_STEP.index(s))
                    if s % UNITS_G == UNITS_G - 1:
                        reciprocals(b, s // UNITS_G)
                    for i, kind, index, rel in body_chunks(s - VECTOR_READS_AFTER, first, last):
                        chunk(b + rel, kind, index, chunk_banks[chunk_bank(i)])
                    for i, kind, index, rel in body_chunks(s - VECTOR_READS_AFTER - 1, first, last):
                        if kind == "r":
                            divide_o(b + rel, index)
                    if s in VECTOR_UNITS:
                        take_pt(b, s)

            def last_part():
                divide_o(B - 1, 2)
                for i, (kind, index) in enumerate(LAST_CHUNKS):
                    if kind == "o":
                        chunk(B - 1, kind, index, chunk_banks[chunk_bank(i)])

            bodies(dve, body, last_part)


OUTPUT = ((B, N, D), "float32")


def kernel(x, adj, L0_gnn_Wq, L0_gnn_Wk, L0_gnn_Wv, L0_gnn_bv, L0_gnn_Wo, L0_gnn_bo):
    import numpy as np
    import concourse.bacc as bacc
    from concourse.bass_utils import run_bass_kernel_spmd

    nc = bacc.Bacc("TRN2", target_bir_lowering=False, num_devices=1)
    given = {"x": x, "adj": adj, "wq": L0_gnn_Wq, "wk": L0_gnn_Wk, "wv": L0_gnn_Wv, "bv": L0_gnn_bv,
             "wo": L0_gnn_Wo, "bo": L0_gnn_bo}
    arrays = {name: np.ascontiguousarray(a) for name, a in given.items()}
    args = [nc.dram_tensor(name, a.shape, mybir.dt.from_np(a.dtype), kind="ExternalInput").ap() for name, a in arrays.items()]
    shape, dtype = OUTPUT
    out = nc.dram_tensor("out", shape, mybir.dt.from_np(np.dtype(dtype)), kind="ExternalOutput").ap()
    build(nc, *args, out)
    return run_bass_kernel_spmd(nc, [arrays], core_ids=[0]).results[0]["out"]
```

```python
from contextlib import ExitStack

import concourse.bass as bass
from concourse import mybir

F32 = mybir.dt.float32
F32R = mybir.dt.float32r
ALU = mybir.AluOpType
ACT = mybir.ActivationFunctionType
AX = mybir.AxisListType

B, N, D = 16, 512, 384
HEADS = 12
HD = D // HEADS
P = 128
SCALE = float(D) ** -0.5
EPS = 1e-5
BIG = 3.0e38

G = D // P
A = P // HD
NT = N // P
HALVES = 2
PER_HALF = NT // HALVES
UNITS = G * HALVES * A * PER_HALF
UNITS_G = UNITS // G
UNITS_H = UNITS_G // HALVES
NHALF = G * HALVES
HN = N // HALVES
BLOCKS = 3
STACK_DMAS = BLOCKS * 2 * A
SLOTS = 3

SCORES_AHEAD = 3
AHEAD = 2

CHUNKS = [
    ((1, 1, 2), "v", 0, 0, 0), ((3, 4, 5), "v", 1, 0, 1), ((6,), "r", 2, -1, 0), ((6, 6, 7), "v", 2, 0, 1), ((7, 8, 9), "v", 3, 0, 0),
    ((10,), "x", 0, 1, 1), ((11,), "x", 1, 1, 0), ((12,), "x", 2, 1, 1),
    ((14, 14, 15), "k", 0, 1, 0), ((16, 17, 18), "q", 0, 1, 1), ((19,), "r", 0, 0, 0), ((20,), "lin", 0, 1, 1),
    ((21, 22, 23), "o", 0, -1, 0), ((24, 24, 25), "o", 1, -1, 1), ((26, 27, 28), "o", 2, -1, 0), ((29, 30, 30), "o", 3, -1, 1),
    ((31, 32, 32), "k", 1, 1, 0), ((33, 34, 35), "q", 1, 1, 1), ((36,), "r", 1, 0, 0), ((37,), "lin", 1, 1, 1),
    ((38, 39, 40), "k", 2, 1, 0), ((41, 42, 43), "q", 2, 1, 1), ((45,), "lin", 2, 1, 0),
]
VECTOR_READS_AFTER = 1
STORE_STEP = [26, 29, 32, 35]
BANKS = 2
SCORE_BANKS = 3
FIRST_CHUNKS = [(kind, index, i % BANKS) for i, (kind, index) in enumerate(
    [("w", i) for i in range(4 * G)] + [("x", t) for t in range(G)] + [(kind, g) for g in range(G) for kind in ("k", "q", "lin")])]
LAST_CHUNKS = [("r", 2, 1)] + [("o", t, t % 2) for t in range(NT)]
PV_STEP = {(UNITS_H * h + 10 + m) % UNITS: (h, m, -((UNITS_H * h + 10 + m) // UNITS)) for h in range(NHALF) for m in range(NT)}
LOAD_X_STEP = 0
ROUND_STEP = [33, 39, 9]
DIVIDE_STEP = [22, 38, 8]
ADJ_SUM_STEP = [4, 8]
VECTOR_UNITS = [u for u in range(UNITS) if u % 5 == 0]


def present(rel, first, last):
    return not (first and rel < 0) and not (last and rel > 0)


def unit(u):
    g, r = divmod(u, UNITS_G)
    half, r = divmod(r, UNITS_H)
    a, n2 = divmod(r, PER_HALF)
    return g, half, a, n2, half * PER_HALF + n2


def before_in_bank(bank, upto, b, first, last):
    for steps, kind, index, rel, own in reversed(CHUNKS[:upto]):
        if own == bank and present(rel, first, last):
            return kind, index, b + rel
    if first:
        return before_in_list(FIRST_CHUNKS, len(FIRST_CHUNKS), bank, 0)
    return [(kind, index, b - 1 + rel) for steps, kind, index, rel, own in CHUNKS if own == bank][-1]


def before_in_list(chunks, upto, bank, b):
    for kind, index, own in reversed(chunks[:upto]):
        if own == bank:
            return kind, index, b
    return None


def wait(engine, semaphore, count):
    if not (isinstance(count, int) and count <= 0):
        engine.wait_ge(semaphore, count)


def wait_apart(engine, semaphore, count, carried, met):
    count = worked_out(engine, count)
    engine.wait_ge(carried, met)
    engine.wait_ge(semaphore, count)


def worked_out(engine, count):
    return count if isinstance(count, int) else engine.to_reg(count)


def vector_evacs(b, u):
    return b * len(VECTOR_UNITS) + sum(v <= u for v in VECTOR_UNITS) - (
        sum(v > UNITS + u for v in VECTOR_UNITS) if u < 0 else 0)


def scalar_evacs(b, u):
    scalar_units = [v for v in range(UNITS) if v not in VECTOR_UNITS]
    return b * len(scalar_units) + sum(v <= u for v in scalar_units) - (
        sum(v > UNITS + u for v in scalar_units) if u < 0 else 0)


def build(nc, x, adj, wq, wk, wv, bv, wo, bo, out):
    with ExitStack() as ctx:
        def sb(name, shape, dt=F32):
            return ctx.enter_context(nc.sbuf_tensor(name, shape, dt))

        def bank(name):
            return ctx.enter_context(nc.psum_tensor(name, [P, N], F32))

        def sem(name):
            return ctx.enter_context(nc.semaphore(name))

        ident = sb("ident", [P, P])
        head_mask = sb("head_mask", [P, P])
        bv_rows, bo_rows = sb("bv_rows", [P, D]), sb("bo_rows", [P, D])
        w_hi, w_lo = sb("w_hi", [P, 4, G, D], F32R), sb("w_lo", [P, 4, G, D], F32R)
        x_rows = sb("x_rows", [P, NT, D])
        resid = sb("resid", [P, NT, D])
        xt_hi, xt_lo = sb("xt_hi", [P, G, N], F32R), sb("xt_lo", [P, G, N], F32R)
        kt_hi, kt_lo = sb("kt_hi", [P, 2, N], F32R), sb("kt_lo", [P, 2, N], F32R)
        qt_hi, qt_lo = sb("qt_hi", [P, 2, N], F32R), sb("qt_lo", [P, 2, N], F32R)
        k_stack = sb("k_stack", [BLOCKS * HD, G, A, N], F32R)
        q_stack = sb("q_stack", [BLOCKS * HD, G, A, N], F32R)
        adj_rows = sb("adj_rows", [P, NT, N])
        v_rows = sb("v_rows", [P, NT, D])
        neg_a = sb("neg_a", [P, SLOTS, N])
        p_rows = sb("p_rows", [P, SLOTS, N])
        pt = sb("pt", [P, 2, A * NT * HN])
        o_cols = sb("o_cols", [P, N])
        ot_hi, ot_lo = sb("ot_hi", [P, G, N], F32R), sb("ot_lo", [P, G, N], F32R)
        y = sb("y", [P, 2, D])
        neg_max, row_sum = sb("neg_max", [P, UNITS]), sb("row_sum", [P, UNITS])
        k_sum = sb("k_sum", [P, G])
        k_sum_heads = sb("k_sum_heads", [P, P], F32R)
        lin_next, lin = sb("lin_next", [P, UNITS]), sb("lin", [P, UNITS])
        adj_sum = sb("adj_sum", [P, NT])
        a_sum = sb("a_sum", [P, UNITS_G])
        max_zero, live = sb("max_zero", [P, UNITS_G]), sb("live", [P, UNITS_G])
        recip, recip_live = sb("recip", [P, UNITS_G]), sb("recip_live", [P, UNITS_G])
        recip_heads = sb("recip_heads", [P, UNITS_G, HD])
        bn, mv, variance = sb("bn", [P, 2, 6]), sb("mv", [P, 2, 2]), sb("variance", [P, 2, 1])
        neg_mean, rstd, minus_half = sb("neg_mean", [P, 2, 1]), sb("rstd", [P, 2, 1]), sb("minus_half", [P, 1])

        score_bank = [bank(f"score_bank{i}") for i in range(SCORE_BANKS)]
        turn_bank = [bank(f"turn_bank{i}") for i in range(2)]
        o_bank = bank("o_bank")
        chunk_banks = [bank(f"chunk_bank{i}") for i in range(BANKS)]

        w_loaded, bias_loaded, x_loaded, resid_loaded = map(sem, ("w_loaded", "bias_loaded", "x_loaded", "resid_loaded"))
        adj_loaded = [sem(f"adj_loaded{t}") for t in range(NT)]
        stack_loaded = [sem(f"stack_loaded{g}") for g in range(G)]
        stored = [sem(f"stored{i}") for i in range(2)]
        ident_ready, mask_cleared, mask_ready = sem("ident_ready"), sem("mask_cleared"), sem("mask_ready")
        w_turned, w_hi_ready, w_lo_ready = sem("w_turned"), sem("w_hi_ready"), sem("w_lo_ready")
        x_turned, x_hi_ready, x_lo_ready = sem("x_turned"), sem("x_hi_ready"), sem("x_lo_ready")
        kq_done, kq_hi_ready, kq_lo_ready = sem("kq_done"), sem("kq_hi_ready"), sem("kq_lo_ready")
        k_sum_ready, lin_done, lin_read = sem("k_sum_ready"), sem("lin_done"), sem("lin_read")
        v_done, v_ready = sem("v_done"), sem("v_ready")
        scores_done, max_done, exp_done = sem("scores_done"), sem("max_done"), sem("exp_done")
        turned, pt_by_vector, pt_by_scalar = sem("turned"), sem("pt_by_vector"), sem("pt_by_scalar")
        pv_done, adj_summed, lin_moved, stats = sem("pv_done"), sem("adj_summed"), sem("lin_moved"), sem("stats")
        recip_ready, r_done, r_ready = sem("recip_ready"), sem("r_done"), sem("r_ready")
        o_ready, o_hi_ready, o_lo_ready = sem("o_ready"), sem("o_hi_ready"), sem("o_lo_ready")
        norm_scalars = sem("norm_scalars")
        proj_done, norm_step, y_ready, resid_ready = sem("proj_done"), sem("norm_step"), sem("y_ready"), sem("resid_ready")

        def pt_tile(h):
            return pt[:, h % 2, :].rearrange("p (a m n) -> p a m n", a=A, m=NT)

        w_rows = pt[:, :, :].rearrange("p b f -> p (b f)")[:, 0:4 * G * D].rearrange("p (w t i) -> p w t i", w=4, t=G)

        def done_chunks(step, first, last):
            for steps, kind, index, rel, bank in CHUNKS:
                if steps[-1] == step and present(rel, first, last):
                    yield kind, index, rel, chunk_banks[bank]

        def ahead(step, lead, last):
            u = step + lead
            if u < UNITS:
                return u, 0
            return (None, 0) if last else (u - UNITS, 1)

        block = ctx.enter_context(nc.Block())

        def bodies(engine, body, last_part):
            body(0, True, False)
            with engine.Fori(1, B - 1) as b:
                body(b, False, False)
            body(B - 1, False, True)
            last_part()

        @block.sync
        def _(sp):
            def load_first_x():
                sp.dma_start(x_rows[:, :, :], x[0:1].rearrange("o (t p) d -> p (o t) d", p=P)).then_inc(x_loaded, 16)

            def load_adj(b, t):
                sp.dma_start(adj_rows[:, t, :], adj[bass.ds(b, 1), t * P:(t + 1) * P, :].rearrange("o p n -> p (o n)")).then_inc(adj_loaded[t], 16)

            def load_half(b, half):
                sp.wait_ge(max_done, UNITS * b + UNITS - UNITS_H * (HALVES - 1 - half))
                for n2 in range(PER_HALF):
                    load_adj(b + 1, half * PER_HALF + n2)

            def load_resid(b):
                stores = worked_out(sp, 16 * (NT // 2) * b)
                wait(sp, norm_step, 4 * NT * b)
                for slot in stored:
                    wait(sp, slot, stores)
                sp.dma_start(resid[:, :, :], x[bass.ds(b, 1)].rearrange("o (t p) d -> p (o t) d", p=P)).then_inc(resid_loaded, 16)

            def stack(b, g):
                parts_made = worked_out(sp, 2 * G * b + 2 * g + 2)
                wait(sp, scores_done, UNITS * (b - 1) + UNITS_G * (g + 1))
                sp.wait_ge(kq_lo_ready, parts_made)
                for a in range(A):
                    own = slice(HD * a, HD * a + HD)
                    for to, parts in ((k_stack, (kt_hi, kt_lo, kt_hi)), (q_stack, (qt_hi, qt_hi, qt_lo))):
                        for j, part in enumerate(parts):
                            sp.dma_start(to[HD * j:HD * j + HD, g, a, :].bitcast(F32), part[own, g % 2, :].bitcast(F32)).then_inc(stack_loaded[g], 16)

            for w, src in enumerate((wq, wk, wv, wo)):
                sp.dma_start(w_rows[:, w, :, :], src.rearrange("(t p) i -> p t i", p=P)).then_inc(w_loaded, 16)
            load_first_x()
            for rows, src in ((bv_rows, bv), (bo_rows, bo)):
                sp.dma_start(rows[:, :], src.rearrange("(o d) -> o d", o=1).broadcast_to([P, D])).then_inc(bias_loaded, 16)
            for t in range(NT):
                load_adj(0, t)
            for g in range(G):
                stack(0, g)

            def body(b, first, last):
                if not last:
                    stack(b + 1, 0)
                load_resid(b)
                if not last:
                    load_half(b, 0)
                    stack(b + 1, 1)
                    load_half(b, 1)
                    stack(b + 1, 2)

            def last_part():
                for slot in stored:
                    sp.wait_ge(slot, 16 * NT // 2 * B)

            bodies(sp, body, last_part)

        @block.gpsimd
        def _(pool):
            nc.gpsimd.memset(ident[:, :], 0.0).then_inc(mask_cleared, 1)
            nc.gpsimd.memset(head_mask[:, :], 0.0).then_inc(mask_cleared, 1)
            nc.gpsimd.memset(minus_half[:, :], -0.5).then_inc(mask_cleared, 1)
            pool.wait_ge(mask_cleared, 3)
            nc.gpsimd.affine_select(out=ident[:, :], in_=ident[:, :], compare_op=ALU.not_equal, fill=1.0, base=0,
                                    pattern=[[-1, P]], channel_multiplier=1).then_inc(ident_ready, 1)
            pool.wait_ge(ident_ready, 1)
            for a in range(A):
                own = slice(HD * a, HD * a + HD)
                if a:
                    pool.wait_ge(mask_ready, a)
                nc.gpsimd.memset(head_mask[own, own], 1.0).then_inc(mask_ready, 1)

            def add_bias(b):
                pool.wait_ge(resid_loaded, 16 * (b + 1))
                nc.gpsimd.tensor_tensor(resid[:, :, :], resid[:, :, :], bo_rows[:, :].unsqueeze(1).broadcast_to([P, NT, D]),
                                        ALU.add).then_inc(resid_ready, 1)

            def spread(b, g):
                wait(pool, r_done, G * b + g)
                wait_apart(pool, stats, 6 * (G * b + g + 1), bias_loaded, 32)
                nc.gpsimd.tensor_copy(recip_heads[:, :, :], recip_live[:, :].unsqueeze(2).broadcast_to([P, UNITS_G, HD])).then_inc(recip_ready, 1)

            def low_part(b, g):
                pool.wait_ge(o_hi_ready, G * b + g + 1)
                nc.gpsimd.tensor_tensor(ot_lo[:, g, :], o_cols[:, :], ot_hi[:, g, :].bitcast(F32), ALU.subtract).then_inc(o_lo_ready, 1)

            def normalise(b, t):
                slot = t % 2
                wait_apart(pool, norm_step, 4 * (NT * b + t + 1), bias_loaded, 32)
                nc.gpsimd.tensor_scalar(neg_mean[:, slot, :], mv[:, slot, 0:1], -1.0, 0.0, ALU.mult, ALU.add).then_inc(norm_scalars, 1)
                nc.gpsimd.tensor_tensor(rstd[:, slot, :], variance[:, slot, :], minus_half[:, :], ALU.pow).then_inc(norm_scalars, 1)
                wait_apart(pool, norm_scalars, 2 * (NT * b + t + 1), bias_loaded, 32)
                nc.gpsimd.tensor_scalar(y[:, slot, :], y[:, slot, :], neg_mean[:, slot, :], rstd[:, slot, :], ALU.add, ALU.mult).then_inc(y_ready, 1)

            pool.wait_ge(mask_ready, A)
            pool.wait_ge(bias_loaded, 32)

            def body(b, first, last):
                if not first:
                    spread(b - 1, 2)
                    low_part(b - 1, 2)
                spread(b, 0)
                if not first:
                    for t in range(NT):
                        normalise(b - 1, t)
                spread(b, 1)
                low_part(b, 0)
                add_bias(b)
                low_part(b, 1)

            def last_part():
                spread(B - 1, 2)
                low_part(B - 1, 2)
                for t in range(NT):
                    normalise(B - 1, t)

            bodies(pool, body, last_part)

        @block.tensor
        def _(pe):
            def turn_w(i, bank):
                w, t = divmod(i, G)
                for s in range(G):
                    last = pe.transpose(bank[:, s * P:(s + 1) * P], w_rows[:, w, s, t * P:(t + 1) * P], ident[:, :])
                last.then_inc(w_turned, 1)

            def turn_x(b, t, bank):
                pe.wait_ge(x_loaded, 16 * (b + 1))
                for s in range(NT):
                    last = pe.transpose(bank[:, s * P:(s + 1) * P], x_rows[:, s, t * P:(t + 1) * P], ident[:, :])
                last.then_inc(x_turned, 1)

            def three_products(dst, pairs, done, piece):
                for n, (lhs, rhs) in enumerate(pairs):
                    if piece in (None, n * G // len(pairs)):
                        last = pe.matmul(dst, lhs, rhs, start=(n == 0), stop=(n == len(pairs) - 1))
                if piece in (None, G - 1):
                    last.then_inc(done, 1)

            def parts(left, left_cols, right, right_cols):
                return [(left[i][:, t, left_cols], right[j][:, t, right_cols])
                        for t in range(G) for i, j in ((0, 0), (0, 1), (1, 0))]

            def weight(w):
                return (w_hi[:, w], w_lo[:, w])

            def project_kq(b, w, g, bank, piece):
                pe.wait_ge(x_lo_ready, G * (b + 1))
                three_products(bank[:, :], parts(weight(w), slice(g * P, (g + 1) * P), (xt_hi, xt_lo), slice(0, N)), kq_done, piece)

            def linear_sums(b, g, bank):
                pe.wait_ge(k_sum_ready, G * b + g + 1)
                pe.wait_ge(kq_lo_ready, 2 * G * b + 2 * g + 2)
                for t in range(NT):
                    rows = slice(t * P, (t + 1) * P)
                    for n, part in enumerate((qt_hi, qt_lo)):
                        last = pe.matmul(bank[:, rows], part[:, g % 2, rows], k_sum_heads[:, :], start=(n == 0), stop=(n == 1))
                last.then_inc(lin_done, 1)

            def project_v(b, t, bank, piece):
                three_products(bank[:, 0:D], parts((xt_hi, xt_lo), slice(t * P, (t + 1) * P), weight(2), slice(0, D)), v_done, piece)

            def project_out(b, t, bank, piece):
                pe.wait_ge(o_lo_ready, G * (b + 1))
                three_products(bank[:, 0:D], parts((ot_hi, ot_lo), slice(t * P, (t + 1) * P), weight(3), slice(0, D)), proj_done, piece)

            def turn_recip(b, g, bank):
                pe.wait_ge(recip_ready, G * b + g + 1)
                for t in range(NT):
                    last = pe.transpose(bank[:, t * P:(t + 1) * P], recip_heads[:, t * A:(t + 1) * A, :].rearrange("p a d -> p (a d)"), ident[:, :])
                last.then_inc(r_done, 1)

            def scores(b, u):
                g, half, a, n2, t = unit(u)
                if u % UNITS_G == 0:
                    pe.wait_ge(stack_loaded[g], 16 * STACK_DMAS * (b + 1))
                wait(pe, max_done, UNITS * b + u + 1 - SCORE_BANKS)
                pe.matmul(score_bank[u % SCORE_BANKS][:, :], q_stack[:, g, a, t * P:(t + 1) * P], k_stack[:, g, a, :],
                          start=True, stop=True).then_inc(scores_done, 1)

            def turn_p(b, u):
                pe.wait_ge(exp_done, UNITS * b + u + 1)
                if (u - 2) % UNITS in VECTOR_UNITS:
                    wait(pe, pt_by_vector, vector_evacs(b, u - 2))
                else:
                    wait(pe, pt_by_scalar, scalar_evacs(b, u - 2))
                for m in range(NT):
                    last = pe.transpose(turn_bank[u % 2][:, m * P:(m + 1) * P], p_rows[:, u % SLOTS, m * P:(m + 1) * P], ident[:, :])
                last.then_inc(turned, 1)

            def weigh_v(b, h, m):
                g, half = divmod(h, HALVES)
                if h == 0:
                    pe.wait_ge(v_ready, NT * b + m + 1)
                if m == 0:
                    if half == 0:
                        wait(pe, o_ready, G * b + g)
                    pe.wait_ge(pt_by_vector, vector_evacs(b, UNITS_H * (h + 1) - 1))
                    pe.wait_ge(pt_by_scalar, scalar_evacs(b, UNITS_H * (h + 1) - 1))
                for a in range(A):
                    head = g * P + a * HD
                    last = pe.matmul(o_bank[a * HD:(a + 1) * HD, half * HN:(half + 1) * HN], v_rows[:, m, head:head + HD],
                                     pt_tile(h)[:, a, m, :], start=(m == 0), stop=(m == NT - 1), tile_position=(0, a * HD))
                if m == NT - 1:
                    last.then_inc(pv_done, 1)

            def chunk(b, kind, index, bank, piece=None):
                if kind == "w":
                    turn_w(index, bank)
                if kind == "x":
                    turn_x(b, index, bank)
                if kind in ("k", "q"):
                    project_kq(b, int(kind == "k"), index, bank, piece)
                if kind == "lin":
                    linear_sums(b, index, bank)
                if kind == "v":
                    project_v(b, index, bank, piece)
                if kind == "o":
                    project_out(b, index, bank, piece)
                if kind == "r":
                    turn_recip(b, index, bank)

            def bank_free(chunk):
                if chunk is not None:
                    kind, index, b = chunk
                    pe.wait_ge(*{
                        "w": (w_lo_ready, index + 1),
                        "x": (x_lo_ready, G * b + index + 1),
                        "k": (kq_lo_ready, 2 * G * b + 2 * index + 1),
                        "q": (kq_lo_ready, 2 * G * b + 2 * index + 2),
                        "lin": (lin_read, G * b + index + 1),
                        "v": (v_ready, NT * b + index + 1),
                        "o": (norm_step, 4 * (NT * b + index) + 1),
                        "r": (r_ready, G * b + index + 1),
                    }[kind])

            pe.wait_ge(ident_ready, 1)
            pe.wait_ge(w_loaded, 64)
            for i, (kind, index, bank) in enumerate(FIRST_CHUNKS):
                bank_free(before_in_list(FIRST_CHUNKS, i, bank, 0))
                if kind == "k" and index == 0:
                    pe.wait_ge(w_lo_ready, 4 * G)
                chunk(0, kind, index, chunk_banks[bank])
            for u in range(SCORES_AHEAD):
                scores(0, u)

            def body(b, first, last):
                for s in range(UNITS):
                    u, rel = ahead(s, SCORES_AHEAD, last)
                    if u is not None:
                        scores(b + rel, u)
                    if s in PV_STEP and present(PV_STEP[s][2], first, last):
                        weigh_v(b + PV_STEP[s][2], *PV_STEP[s][0:2])
                    turn_p(b, s)
                    for i, (steps, kind, index, rel, bank) in enumerate(CHUNKS):
                        if s in steps and present(rel, first, last):
                            if s == steps[0]:
                                bank_free(before_in_bank(bank, i, b, first, last))
                            for piece, at in enumerate(steps):
                                if at == s:
                                    chunk(b + rel, kind, index, chunk_banks[bank], piece if len(steps) > 1 else None)

            def last_part():
                for m in range(NT):
                    weigh_v(B - 1, NHALF - 1, m)
                for i, (kind, index, bank) in enumerate(LAST_CHUNKS):
                    bank_free(before_in_list(LAST_CHUNKS, i, bank, B - 1) or before_in_bank(bank, len(CHUNKS), B - 1, False, True))
                    chunk(B - 1, kind, index, chunk_banks[bank])

            bodies(pe, body, last_part)

        @block.scalar
        def _(act):
            def exponential(b, u):
                act.wait_ge(max_done, UNITS * b + u + 1)
                wait(act, turned, UNITS * b + u + 1 - SLOTS)
                nc.scalar.activation(p_rows[:, u % SLOTS, :], neg_a[:, u % SLOTS, :], ACT.Exp, bias=neg_max[:, u:u + 1],
                                     scale=-1.0, accum_out=row_sum[:, u:u + 1]).then_inc(exp_done, 1)

            def chunk(b, kind, index, bank):
                if kind == "w":
                    w, t = divmod(index, G)
                    act.wait_ge(w_turned, index + 1)
                    nc.scalar.activation(w_hi[:, w, t, :], bank[:, 0:D], ACT.Copy, scale=SCALE if w == 0 else 1.0).then_inc(w_hi_ready, 1)
                if kind == "x":
                    act.wait_ge(x_turned, G * b + index + 1)
                    nc.scalar.activation(xt_hi[:, index, :], bank[:, :], ACT.Copy).then_inc(x_hi_ready, 1)
                if kind in ("k", "q"):
                    act.wait_ge(kq_done, 2 * G * b + 2 * index + 1 + (kind == "q"))
                    if kind == "k":
                        wait(act, stack_loaded[{0: 2, 1: 1, 2: 0}[index]], 16 * STACK_DMAS * (b + (index == 2)))
                        nc.scalar.activation(kt_hi[:, index % 2, :], bank[:, :], ACT.Copy, accum_out=k_sum[:, index:index + 1]).then_inc(kq_hi_ready, 1)
                    else:
                        nc.scalar.activation(qt_hi[:, index % 2, :], bank[:, :], ACT.Copy).then_inc(kq_hi_ready, 1)
                if kind == "r":
                    act.wait_ge(r_done, G * b + index + 1)
                    wait(act, o_lo_ready, G * b + index)
                    nc.scalar.activation(o_cols[:, :], bank[:, :], ACT.Copy).then_inc(r_ready, 1)

            def round_o(b, g):
                act.wait_ge(o_ready, G * b + g + 1)
                if g == 0:
                    wait(act, proj_done, NT * b)
                nc.scalar.activation(ot_hi[:, g, :], o_cols[:, :], ACT.Copy).then_inc(o_hi_ready, 1)

            def take_pt(b, u):
                g, half, a, n2, t = unit(u)
                h = g * HALVES + half
                act.wait_ge(turned, UNITS * b + u + 1)
                wait(act, pv_done, NHALF * b + h - 1)
                nc.scalar.activation(pt_tile(h)[:, a, :, n2 * P:(n2 + 1) * P],
                                     turn_bank[u % 2][:, :].rearrange("p (m n) -> p m n", m=NT), ACT.Copy).then_inc(pt_by_scalar, 1)

            def store(b, t):
                act.wait_ge(y_ready, NT * b + t + 1)
                act.dma_start(out[bass.ds(b, 1), t * P:(t + 1) * P, :].rearrange("o p d -> p (o d)"), y[:, t % 2, :]).then_inc(stored[t % 2], 16)

            def load_x(b):
                wait(act, x_turned, G * b)
                act.dma_start(x_rows[:, :, :], x[bass.ds(b, 1)].rearrange("o (t p) d -> p (o t) d", p=P)).then_inc(x_loaded, 16)

            for kind, index, bank in FIRST_CHUNKS:
                chunk(0, kind, index, chunk_banks[bank])
            for u in range(AHEAD):
                exponential(0, u)

            def body(b, first, last):
                for s in range(UNITS):
                    u, rel = ahead(s, AHEAD, last)
                    if u is not None:
                        exponential(b + rel, u)
                    if s == LOAD_X_STEP and not last:
                        load_x(b + 1)
                    if s not in VECTOR_UNITS:
                        take_pt(b, s)
                    for kind, index, rel, bank in done_chunks(s, first, last):
                        chunk(b + rel, kind, index, bank)
                    if s in ROUND_STEP and not (first and s == ROUND_STEP[2]):
                        g = ROUND_STEP.index(s)
                        round_o(b - (g == 2), g)
                    if s in STORE_STEP and not first:
                        store(b - 1, STORE_STEP.index(s))

            def last_part():
                chunk(B - 1, "r", 2, chunk_banks[1])
                round_o(B - 1, 2)
                for t in range(NT):
                    store(B - 1, t)

            bodies(act, body, last_part)

        @block.vector
        def _(dve):
            def row_max(b, u):
                g, half, a, n2, t = unit(u)
                if u in (0, 1, UNITS_H, UNITS_H + 1):
                    dve.wait_ge(adj_loaded[t], 16 * (b + 1))
                wait(dve, exp_done, UNITS * b + u + 1 - SLOTS)
                wait_apart(dve, scores_done, UNITS * b + u + 1, adj_loaded[t], 16)
                nc.vector.tensor_tensor_reduce(neg_a[:, u % SLOTS, :], score_bank[u % SCORE_BANKS][:, :], adj_rows[:, t, :], -1.0, BIG,
                                               ALU.add, ALU.min, neg_max[:, u:u + 1]).then_inc(max_done, 1)

            def chunk(b, kind, index, bank):
                if kind == "w":
                    w, t = divmod(index, G)
                    dve.wait_ge(w_hi_ready, index + 1)
                    nc.vector.scalar_tensor_tensor(w_lo[:, w, t, :], bank[:, 0:D], SCALE if w == 0 else 1.0,
                                                   w_hi[:, w, t, :].bitcast(F32), ALU.mult, ALU.subtract).then_inc(w_lo_ready, 1)
                if kind == "x":
                    dve.wait_ge(x_hi_ready, G * b + index + 1)
                    nc.vector.tensor_tensor(xt_lo[:, index, :], bank[:, :], xt_hi[:, index, :].bitcast(F32), ALU.subtract).then_inc(x_lo_ready, 1)
                if kind in ("k", "q"):
                    hi, lo = (kt_hi, kt_lo) if kind == "k" else (qt_hi, qt_lo)
                    dve.wait_ge(kq_hi_ready, 2 * G * b + 2 * index + 1 + (kind == "q"))
                    if kind == "k":
                        wait(dve, lin_done, G * b + index)
                        nc.vector.tensor_scalar(k_sum_heads[:, :], head_mask[:, :], k_sum[:, index:index + 1], None, ALU.mult).then_inc(k_sum_ready, 1)
                    nc.vector.tensor_tensor(lo[:, index % 2, :], bank[:, :], hi[:, index % 2, :].bitcast(F32), ALU.subtract).then_inc(kq_lo_ready, 1)
                if kind == "lin":
                    dve.wait_ge(lin_done, G * b + index + 1)
                    of_heads = bank[:, :].rearrange("p (h n a d) -> p h a n d", h=HALVES, n=PER_HALF, a=A)[:, :, :, :, 0]
                    nc.vector.tensor_copy(lin_next[:, index * UNITS_G:(index + 1) * UNITS_G].rearrange("p (h a n) -> p h a n", h=HALVES, a=A),
                                          of_heads).then_inc(lin_read, 1)
                if kind == "v":
                    dve.wait_ge(v_done, NT * b + index + 1)
                    nc.vector.tensor_tensor(v_rows[:, index, :], bank[:, 0:D], bv_rows[:, :], ALU.add).then_inc(v_ready, 1)
                if kind == "o":
                    residual_norm(b, index, bank)

            def residual_norm(b, t, bank):
                done = 4 * (NT * b + t)
                slot = t % 2
                dve.wait_ge(proj_done, NT * b + t + 1)
                dve.wait_ge(resid_ready, b + 1)
                if t >= 2:
                    dve.wait_ge(stored[slot], 16 * (NT // 2 * b + t // 2))
                nc.vector.tensor_tensor(y[:, slot, :], bank[:, 0:D], resid[:, t, :], ALU.add).then_inc(norm_step, 1)
                dve.wait_ge(norm_step, done + 1)
                nc.vector.bn_stats(bn[:, slot, :], y[:, slot, :]).then_inc(norm_step, 1)
                wait_apart(dve, norm_step, done + 2, norm_step, 1)
                nc.vector.bn_aggr(mv[:, slot, :], bn[:, slot, :]).then_inc(norm_step, 1)
                dve.wait_ge(norm_step, done + 3)
                nc.vector.tensor_scalar(variance[:, slot, :], mv[:, slot, 1:2], EPS, None, ALU.add).then_inc(norm_step, 1)

            def sum_adj(b, half):
                nc.vector.tensor_reduce(adj_sum[:, half * PER_HALF:(half + 1) * PER_HALF],
                                        adj_rows[:, half * PER_HALF:(half + 1) * PER_HALF, :], AX.X, ALU.add).then_inc(adj_summed, 1)

            def move_lin(b):
                dve.wait_ge(lin_read, G * (b + 1))
                nc.vector.tensor_copy(lin[:, :], lin_next[:, :]).then_inc(lin_moved, 1)

            def reciprocals(b, g):
                cols = slice(g * UNITS_G, (g + 1) * UNITS_G)
                done = 6 * (G * b + g)

                def heads(ap):
                    return ap.rearrange("p (h a n) -> p h a n", h=HALVES, a=A)

                dve.wait_ge(exp_done, UNITS * b + (g + 1) * UNITS_G)
                dve.wait_ge(lin_moved, b + 1)
                dve.wait_ge(adj_summed, HALVES * (b + 1))
                nc.vector.tensor_tensor(heads(a_sum[:, :]), heads(lin[:, cols]),
                                        adj_sum[:, :].rearrange("p (h n) -> p h n", h=HALVES).unsqueeze(2).broadcast_to([P, HALVES, A, PER_HALF]),
                                        ALU.add).then_inc(stats, 1)
                nc.vector.tensor_scalar(max_zero[:, :], neg_max[:, cols], 0.0, None, ALU.is_equal).then_inc(stats, 1)
                nc.vector.reciprocal(recip[:, :], row_sum[:, cols]).then_inc(stats, 1)
                dve.wait_ge(stats, done + 2)
                nc.vector.scalar_tensor_tensor(live[:, :], a_sum[:, :], 0.0, max_zero[:, :], ALU.is_equal, ALU.mult).then_inc(stats, 1)
                dve.wait_ge(stats, done + 4)
                nc.vector.tensor_scalar(live[:, :], live[:, :], -1.0, 1.0, ALU.mult, ALU.add).then_inc(stats, 1)
                dve.wait_ge(stats, done + 5)
                wait(dve, recip_ready, G * b + g)
                nc.vector.tensor_tensor(recip_live[:, :].rearrange("p (h n a) -> p h a n", h=HALVES, a=A), heads(recip[:, :]),
                                        heads(live[:, :]), ALU.mult).then_inc(stats, 1)

            def divide_o(b, g):
                dve.wait_ge(r_ready, G * b + g + 1)
                dve.wait_ge(pv_done, NHALF * b + (g + 1) * HALVES)
                nc.vector.tensor_tensor(o_cols[:, :], o_bank[:, :], o_cols[:, :], ALU.mult).then_inc(o_ready, 1)

            def take_pt(b, u):
                g, half, a, n2, t = unit(u)
                h = g * HALVES + half
                dve.wait_ge(turned, UNITS * b + u + 1)
                wait(dve, pv_done, NHALF * b + h - 1)
                nc.vector.tensor_copy(pt_tile(h)[:, a, :, n2 * P:(n2 + 1) * P],
                                      turn_bank[u % 2][:, :].rearrange("p (m n) -> p m n", m=NT)).then_inc(pt_by_vector, 1)

            dve.wait_ge(mask_ready, A)
            dve.wait_ge(bias_loaded, 32)
            for kind, index, bank in FIRST_CHUNKS:
                chunk(0, kind, index, chunk_banks[bank])
            for u in range(AHEAD):
                row_max(0, u)

            def body(b, first, last):
                for s in range(UNITS):
                    u, rel = ahead(s, AHEAD, last)
                    if u is not None:
                        row_max(b + rel, u)
                    if s == 0:
                        move_lin(b)
                    if s in ADJ_SUM_STEP:
                        sum_adj(b, ADJ_SUM_STEP.index(s))
                    if s % UNITS_G == UNITS_G - 1:
                        reciprocals(b, s // UNITS_G)
                    for kind, index, rel, bank in done_chunks(s - VECTOR_READS_AFTER, first, last):
                        chunk(b + rel, kind, index, bank)
                    if s in DIVIDE_STEP and not (first and s == DIVIDE_STEP[2]):
                        g = DIVIDE_STEP.index(s)
                        divide_o(b - (g == 2), g)
                    if s in VECTOR_UNITS:
                        take_pt(b, s)

            def last_part():
                divide_o(B - 1, 2)
                for kind, index, bank in LAST_CHUNKS:
                    if kind == "o":
                        chunk(B - 1, kind, index, chunk_banks[bank])

            bodies(dve, body, last_part)


OUTPUT = ((B, N, D), "float32")


def kernel(x, adj, L0_gnn_Wq, L0_gnn_Wk, L0_gnn_Wv, L0_gnn_bv, L0_gnn_Wo, L0_gnn_bo):
    import numpy as np
    import concourse.bacc as bacc
    from concourse.bass_utils import run_bass_kernel_spmd

    nc = bacc.Bacc("TRN2", target_bir_lowering=False, num_devices=1)
    given = {"x": x, "adj": adj, "wq": L0_gnn_Wq, "wk": L0_gnn_Wk, "wv": L0_gnn_Wv, "bv": L0_gnn_bv,
             "wo": L0_gnn_Wo, "bo": L0_gnn_bo}
    arrays = {name: np.ascontiguousarray(a) for name, a in given.items()}
    args = [nc.dram_tensor(name, a.shape, mybir.dt.from_np(a.dtype), kind="ExternalInput").ap() for name, a in arrays.items()]
    shape, dtype = OUTPUT
    out = nc.dram_tensor("out", shape, mybir.dt.from_np(np.dtype(dtype)), kind="ExternalOutput").ap()
    build(nc, *args, out)
    return run_bass_kernel_spmd(nc, [arrays], core_ids=[0]).results[0]["out"]
```

```python
from contextlib import ExitStack

import concourse.bass as bass
from concourse import mybir

F32 = mybir.dt.float32
F32R = mybir.dt.float32r
ALU = mybir.AluOpType
ACT = mybir.ActivationFunctionType
AX = mybir.AxisListType

B, N, D = 16, 512, 384
HEADS = 12
HD = D // HEADS
P = 128
SCALE = float(D) ** -0.5
EPS = 1e-5
BIG = 3.0e38

G = D // P
A = P // HD
NT = N // P
HALVES = 2
PER_HALF = NT // HALVES
UNITS = G * HALVES * A * PER_HALF
UNITS_G = UNITS // G
UNITS_H = UNITS_G // HALVES
NHALF = G * HALVES
HN = N // HALVES
BLOCKS = 3
STACK_DMAS = BLOCKS * 2
SLOTS = 4

SCORES_AHEAD = 3
AHEAD = 2

MIDDLE_BODY = [
    ((0, 2, 3), "v", 0, 0, 0), ((4, 5, 5), "v", 1, 0, 1), ((6,), "r", 2, -1, 0), ((7, 7, 8), "v", 2, 0, 1),
    ((8, 9, 10), "v", 3, 0, 0), ((10,), "x", 0, 1, 1), ((12,), "x", 1, 1, 0), ((12,), "x", 2, 1, 1), ((14, 15, 15), "k", 0, 1, 0),
    ((16, 18, 19), "q", 0, 1, 1), ((20,), "r", 0, 0, 0), ((21,), "lin", 0, 1, 1), ((21, 23, 23), "o", 0, -1, 0),
    ((24, 24, 25), "o", 1, -1, 1), ((26, 26, 28), "o", 2, -1, 0), ((29, 29, 29), "o", 3, -1, 1), ((29, 30, 32), "k", 1, 1, 0),
    ((34, 35, 35), "q", 1, 1, 1), ((36,), "r", 1, 0, 0), ((39,), "lin", 1, 1, 1), ((38, 38, 41), "k", 2, 1, 0),
    ((41, 41, 43), "q", 2, 1, 1), ((46,), "lin", 2, 1, 0),
]
FIRST_BODY = [
    ((0, 0, 1), "v", 0, 0, 1), ((2, 2, 3), "v", 1, 0, 1), ((2, 4, 4), "v", 2, 0, 0), ((4, 5, 5), "v", 3, 0, 1),
    ((7, 8, 9), "k", 2, 0, 0), ((7, 8, 10), "q", 2, 0, 1), ((13,), "lin", 2, 0, 0), ((15,), "x", 0, 1, 1), ((16,), "x", 1, 1, 0),
    ((16,), "x", 2, 1, 1), ((20,), "r", 0, 0, 0), ((20, 22, 22), "k", 0, 1, 1), ((23, 24, 24), "q", 0, 1, 0),
    ((26,), "lin", 0, 1, 1), ((28, 29, 30), "k", 1, 1, 0), ((31, 32, 33), "q", 1, 1, 1), ((35,), "lin", 1, 1, 0),
    ((39,), "r", 1, 0, 1), ((38, 39, 40), "k", 2, 1, 0), ((41, 43, 43), "q", 2, 1, 1), ((46,), "lin", 2, 1, 0),
]
LAST_BODY = [
    ((0, 1, 2), "v", 0, 0, 1), ((4, 6, 6), "v", 1, 0, 1), ((6,), "r", 2, -1, 0), ((7, 7, 8), "v", 2, 0, 1),
    ((8, 9, 10), "v", 3, 0, 0), ((20,), "r", 0, 0, 1), ((21, 22, 22), "o", 0, -1, 1), ((24, 24, 25), "o", 1, -1, 0),
    ((27, 28, 29), "o", 2, -1, 0), ((30, 31, 31), "o", 3, -1, 1), ((38,), "r", 1, 0, 0),
]
VECTOR_READS_AFTER = 1
STORE_STEP = [27, 30, 33, 35]
BANKS = 2
SCORE_BANKS = 3
FIRST_CHUNKS = [(kind, index, i % (BANKS + 3)) for i, (kind, index) in enumerate(
    [("w", i) for i in range(G)] + [("x", t) for t in range(G)] + [("w", G + i) for i in range(G)] +
    [("k", 0), ("q", 0), ("k", 1), ("q", 1), ("lin", 0), ("lin", 1)] + [("w", 2 * G + i) for i in range(2 * G)])]
PV_AT = [10, 12, 13, 13]
MOVE_LIN_STEP = 16
RECIP_STEP = [15, 33, 47]
LOAD_X_STEP = 2
ROUND_STEP = [34, 42, 7]
DIVIDE_STEP = [21, 40, 8]
ADJ_SUM_STEP = [8, 11]
VECTOR_UNITS = [0, 4, 9, 12, 13, 15, 18, 20, 22, 26, 30, 32, 35, 37, 39, 42, 43, 45, 47]
LAST_VECTOR_UNITS = [1, 2, 4, 9, 11, 12, 17, 18, 20, 22, 24, 26, 27, 30, 34, 36, 37, 40, 42, 44, 46, 47]


def chunks_of(first, last):
    return FIRST_BODY if first else LAST_BODY if last else MIDDLE_BODY


def pv_pieces(step, first):
    pieces = [(h, m, -((UNITS_H * h + at) // UNITS)) for h in range(NHALF) for m, at in enumerate(PV_AT)
              if (UNITS_H * h + at) % UNITS == step]
    return [piece for piece in pieces if not (first and piece[2] < 0)]


def unit(u):
    g, r = divmod(u, UNITS_G)
    half, r = divmod(r, UNITS_H)
    a, n2 = divmod(r, PER_HALF)
    return g, half, a, n2, half * PER_HALF + n2


def before_in_bank(bank, upto, b, first, last):
    for steps, kind, index, rel, own in reversed(chunks_of(first, last)[:upto]):
        if own == bank:
            return kind, index, b + rel
    if first:
        return before_in_list(FIRST_CHUNKS, len(FIRST_CHUNKS), bank, 0)
    return [(kind, index, b - 1 + rel) for steps, kind, index, rel, own in MIDDLE_BODY if own == bank][-1]


def before_in_list(chunks, upto, bank, b):
    for kind, index, own in reversed(chunks[:upto]):
        if own == bank:
            return kind, index, b
    return None


def wait(engine, semaphore, count):
    if not (isinstance(count, int) and count <= 0):
        engine.wait_ge(semaphore, count)


def wait_apart(engine, semaphore, count, carried, met):
    count = worked_out(engine, count)
    engine.wait_ge(carried, met)
    engine.wait_ge(semaphore, count)


def worked_out(engine, count):
    return count if isinstance(count, int) else engine.to_reg(count)


def vector_units(b):
    return LAST_VECTOR_UNITS if isinstance(b, int) and b == B - 1 else VECTOR_UNITS


def evacs(b, u, regular, own):
    return b * len(regular) + sum(v <= u for v in own) - (sum(v > UNITS + u for v in regular) if u < 0 else 0)


def others(units):
    return [u for u in range(UNITS) if u not in units]


def vector_evacs(b, u):
    return evacs(b, u, VECTOR_UNITS, vector_units(b))


def scalar_evacs(b, u):
    return evacs(b, u, others(VECTOR_UNITS), others(vector_units(b)))


def build(nc, x, adj, wq, wk, wv, bv, wo, bo, out):
    with ExitStack() as ctx:
        def sb(name, shape, dt=F32):
            return ctx.enter_context(nc.sbuf_tensor(name, shape, dt))

        def bank(name):
            return ctx.enter_context(nc.psum_tensor(name, [P, N], F32))

        def sem(name):
            return ctx.enter_context(nc.semaphore(name))

        ident = sb("ident", [P, P])
        head_mask = sb("head_mask", [P, P])
        bv_rows, bo_rows = sb("bv_rows", [P, D]), sb("bo_rows", [P, D])
        w_hi, w_lo = sb("w_hi", [P, 4, G, D], F32R), sb("w_lo", [P, 4, G, D], F32R)
        x_rows = sb("x_rows", [P, NT, D])
        resid = sb("resid", [P, NT, D])
        xt_hi, xt_lo = sb("xt_hi", [P, G, N], F32R), sb("xt_lo", [P, G, N], F32R)
        kt_hi, kt_lo = sb("kt_hi", [P, G, N], F32R), sb("kt_lo", [P, G, N], F32R)
        qt_hi, qt_lo = sb("qt_hi", [P, G, N], F32R), sb("qt_lo", [P, G, N], F32R)
        k_stack = sb("k_stack", [BLOCKS * HD, G, A, N], F32R)
        q_stack = sb("q_stack", [BLOCKS * HD, G, A, N], F32R)
        adj_rows = sb("adj_rows", [P, NT, N])
        v_rows = sb("v_rows", [P, NT, D])
        p_rows = sb("p_rows", [P, SLOTS, N])
        pt = sb("pt", [P, 2, A * NT * HN])
        o_cols = sb("o_cols", [P, N])
        ot_hi, ot_lo = sb("ot_hi", [P, G, N], F32R), sb("ot_lo", [P, G, N], F32R)
        neg_max, row_sum = sb("neg_max", [P, UNITS]), sb("row_sum", [P, UNITS])
        k_sum = sb("k_sum", [P, G])
        k_sum_heads = sb("k_sum_heads", [P, P], F32R)
        lin_next, lin = sb("lin_next", [P, UNITS]), sb("lin", [P, UNITS])
        adj_sum = sb("adj_sum", [P, NT])
        max_zero, live = sb("max_zero", [P, UNITS_G]), sb("live", [P, UNITS_G])
        recip, recip_live = sb("recip", [P, UNITS_G]), sb("recip_live", [P, UNITS_G])
        recip_heads = sb("recip_heads", [P, UNITS_G, HD])
        bn, mv, variance = sb("bn", [P, NT, 6]), sb("mv", [P, NT, 2]), sb("variance", [P, NT, 1])
        neg_mean, rstd, minus_half = sb("neg_mean", [P, NT, 1]), sb("rstd", [P, NT, 1]), sb("minus_half", [P, 1])

        score_bank = [bank(f"score_bank{i}") for i in range(SCORE_BANKS)]
        turn_bank = [bank(f"turn_bank{i}") for i in range(2)]
        o_bank = bank("o_bank")
        chunk_banks = [bank(f"chunk_bank{i}") for i in range(BANKS)]

        w_loaded = [sem(f"w_loaded{w}") for w in range(4)]
        bias_loaded, x_loaded, resid_loaded = map(sem, ("bias_loaded", "x_loaded", "resid_loaded"))
        adj_loaded = [sem(f"adj_loaded{t}") for t in range(NT)]
        stack_loaded = [[sem(f"stack_loaded{g}_{a}") for a in range(A)] for g in range(G)]
        stored = sem("stored")
        ident_ready, mask_cleared, mask_ready = sem("ident_ready"), sem("mask_cleared"), sem("mask_ready")
        w_turned, w_hi_ready, w_lo_ready = sem("w_turned"), sem("w_hi_ready"), sem("w_lo_ready")
        x_turned, x_hi_ready, x_lo_ready = sem("x_turned"), sem("x_hi_ready"), sem("x_lo_ready")
        kq_done, kq_hi_ready, kq_lo_ready = sem("kq_done"), sem("kq_hi_ready"), sem("kq_lo_ready")
        k_sum_ready, lin_done, lin_read = sem("k_sum_ready"), sem("lin_done"), sem("lin_read")
        v_done, v_ready = sem("v_done"), sem("v_ready")
        scores_done, max_done, exp_done = sem("scores_done"), sem("max_done"), sem("exp_done")
        turned, pt_by_vector, pt_by_scalar = sem("turned"), sem("pt_by_vector"), sem("pt_by_scalar")
        pv_done, adj_summed, lin_moved, stats = sem("pv_done"), sem("adj_summed"), sem("lin_moved"), sem("stats")
        recip_made, recip_ready, r_done, r_ready = sem("recip_made"), sem("recip_ready"), sem("r_done"), sem("r_ready")
        o_ready, o_hi_ready, o_lo_ready = sem("o_ready"), sem("o_hi_ready"), sem("o_lo_ready")
        norm_scalars = sem("norm_scalars")
        proj_done, norm_step, y_ready, resid_ready = sem("proj_done"), sem("norm_step"), sem("y_ready"), sem("resid_ready")

        def pt_tile(h):
            return pt[:, h % 2, :].rearrange("p (a m n) -> p a m n", a=A, m=NT)

        w_rows = pt[:, :, :].rearrange("p b f -> p (b f)")[:, 0:4 * G * D].rearrange("p (w t i) -> p w t i", w=4, t=G)

        def done_chunks(step, first, last):
            for steps, kind, index, rel, bank in chunks_of(first, last):
                if steps[-1] == step:
                    yield kind, index, rel, chunk_banks[bank]

        def ahead(step, lead, last):
            u = step + lead
            if u < UNITS:
                return u, 0
            return (None, 0) if last else (u - UNITS, 1)

        first_banks = chunk_banks + turn_bank + [o_bank]
        last_banks = [chunk_banks[0]] + score_bank

        block = ctx.enter_context(nc.Block())

        def bodies(engine, body, last_part):
            body(0, True, False)
            with engine.Fori(1, B - 1) as b:
                body(b, False, False)
            body(B - 1, False, True)
            last_part()

        @block.sync
        def _(sp):
            def load_adj(b, t):
                sp.dma_start(adj_rows[:, t, :], adj[bass.ds(b, 1), t * P:(t + 1) * P, :].rearrange("o p n -> p (o n)")).then_inc(adj_loaded[t], 16)

            def load_half(b, half):
                sp.wait_ge(max_done, UNITS * b + UNITS - UNITS_H * (HALVES - 1 - half))
                for n2 in range(PER_HALF):
                    load_adj(b + 1, half * PER_HALF + n2)

            def load_resid(b):
                stores = worked_out(sp, 16 * NT * b)
                wait(sp, norm_step, 3 * NT * b)
                wait(sp, stored, stores)
                sp.dma_start(resid[:, :, :], x[bass.ds(b, 1)].rearrange("o (t p) d -> p (o t) d", p=P)).then_inc(resid_loaded, 16)

            def stack_head(g, a, to, parts):
                own = slice(HD * a, HD * a + HD)
                for j, part in enumerate(parts):
                    sp.dma_start(to[HD * j:HD * j + HD, g, a, :].bitcast(F32), part[own, g, :].bitcast(F32)).then_inc(stack_loaded[g][a], 16)

            def stack_k(g, a):
                stack_head(g, a, k_stack, (kt_hi, kt_lo, kt_hi))

            def stack_q(g, a):
                stack_head(g, a, q_stack, (qt_hi, qt_hi, qt_lo))

            def stack(b, g):
                parts_made = worked_out(sp, 2 * G * b + 2 * g + 2)
                wait(sp, scores_done, UNITS * (b - 1) + UNITS_G * (g + 1))
                sp.wait_ge(kq_lo_ready, parts_made)
                for a in range(A):
                    stack_k(g, a)
                    stack_q(g, a)

            def first_stack():
                sp.wait_ge(kq_lo_ready, 1)
                for a in range(2):
                    stack_k(0, a)
                sp.wait_ge(kq_lo_ready, 2)
                for a in range(A):
                    if a >= 2:
                        stack_k(0, a)
                    stack_q(0, a)

            def load_w(w, src):
                sp.dma_start(w_rows[:, w, :, :], src.rearrange("(t p) i -> p t i", p=P)).then_inc(w_loaded[w], 16)

            load_w(0, wk)
            load_w(1, wq)
            load_adj(0, 0)
            load_w(2, wv)
            load_w(3, wo)
            for rows, src in ((bv_rows, bv), (bo_rows, bo)):
                sp.dma_start(rows[:, :], src.rearrange("(o d) -> o d", o=1).broadcast_to([P, D])).then_inc(bias_loaded, 16)
            for t in range(1, NT):
                load_adj(0, t)
            first_stack()
            for g in range(1, G):
                stack(0, g)

            def body(b, first, last):
                if not last:
                    stack(b + 1, 0)
                load_resid(b)
                if not last:
                    load_half(b, 0)
                    stack(b + 1, 1)
                    load_half(b, 1)
                    stack(b + 1, 2)

            def last_part():
                sp.wait_ge(stored, 16 * NT * B)

            bodies(sp, body, last_part)

        @block.gpsimd
        def _(pool):
            nc.gpsimd.memset(ident[:, :], 0.0).then_inc(mask_cleared, 1)
            nc.gpsimd.memset(head_mask[:, :], 0.0).then_inc(mask_cleared, 1)
            nc.gpsimd.memset(minus_half[:, :], -0.5).then_inc(mask_cleared, 1)
            pool.wait_ge(mask_cleared, 3)
            nc.gpsimd.affine_select(out=ident[:, :], in_=ident[:, :], compare_op=ALU.not_equal, fill=1.0, base=0,
                                    pattern=[[-1, P]], channel_multiplier=1).then_inc(ident_ready, 1)
            pool.wait_ge(ident_ready, 1)
            for a in range(A):
                own = slice(HD * a, HD * a + HD)
                if a:
                    pool.wait_ge(mask_ready, a)
                nc.gpsimd.memset(head_mask[own, own], 1.0).then_inc(mask_ready, 1)

            def add_bias(b):
                pool.wait_ge(resid_loaded, 16 * (b + 1))
                nc.gpsimd.tensor_tensor(resid[:, :, :], resid[:, :, :], bo_rows[:, :].unsqueeze(1).broadcast_to([P, NT, D]),
                                        ALU.add).then_inc(resid_ready, 1)

            def spread(b, g):
                cols = slice(g * UNITS_G, (g + 1) * UNITS_G)
                done = 6 * (G * b + g)

                def heads(ap):
                    return ap.rearrange("p (h a n) -> p h a n", h=HALVES, a=A)

                pool.wait_ge(recip_made, G * b + g + 1)
                pool.wait_ge(lin_moved, b + 1)
                pool.wait_ge(adj_summed, HALVES * (b + 1))
                nc.gpsimd.tensor_tensor(heads(live[:, :]), heads(lin[:, cols]),
                                        adj_sum[:, :].rearrange("p (h n) -> p h n", h=HALVES).unsqueeze(2).broadcast_to([P, HALVES, A, PER_HALF]),
                                        ALU.add).then_inc(stats, 1)
                wait_apart(pool, stats, done + 1, bias_loaded, 32)
                nc.gpsimd.tensor_scalar(live[:, :], live[:, :], 0.0, None, ALU.is_equal).then_inc(stats, 1)
                nc.gpsimd.tensor_scalar(max_zero[:, :], neg_max[:, cols], 0.0, -1.0, ALU.is_equal, ALU.mult).then_inc(stats, 1)
                pool.wait_ge(stats, done + 3)
                nc.gpsimd.tensor_tensor(live[:, :], live[:, :], max_zero[:, :], ALU.mult).then_inc(stats, 1)
                wait_apart(pool, stats, done + 4, bias_loaded, 32)
                nc.gpsimd.tensor_scalar(live[:, :], live[:, :], 1.0, None, ALU.add).then_inc(stats, 1)
                pool.wait_ge(stats, done + 5)
                nc.gpsimd.tensor_tensor(recip_live[:, :].rearrange("p (h n a) -> p h a n", h=HALVES, a=A), heads(recip[:, :]),
                                        heads(live[:, :]), ALU.mult).then_inc(stats, 1)
                wait(pool, r_done, G * b + g)
                wait_apart(pool, stats, done + 6, bias_loaded, 32)
                nc.gpsimd.tensor_copy(recip_heads[:, :, :], recip_live[:, :].unsqueeze(2).broadcast_to([P, UNITS_G, HD])).then_inc(recip_ready, 1)

            def low_part(b, g):
                pool.wait_ge(o_hi_ready, G * b + g + 1)
                nc.gpsimd.tensor_tensor(ot_lo[:, g, :], o_cols[:, :], ot_hi[:, g, :].bitcast(F32), ALU.subtract).then_inc(o_lo_ready, 1)

            def normalise(b, t):
                wait_apart(pool, norm_step, 3 * (NT * b + t + 1), bias_loaded, 32)
                nc.gpsimd.tensor_scalar(neg_mean[:, t, :], mv[:, t, 0:1], -1.0, 0.0, ALU.mult, ALU.add).then_inc(norm_scalars, 1)
                nc.gpsimd.tensor_scalar(variance[:, t, :], mv[:, t, 1:2], EPS, None, ALU.add).then_inc(norm_scalars, 1)
                pool.wait_ge(norm_scalars, 3 * (NT * b + t) + 2)
                nc.gpsimd.tensor_tensor(rstd[:, t, :], variance[:, t, :], minus_half[:, :], ALU.pow).then_inc(norm_scalars, 1)
                wait_apart(pool, norm_scalars, 3 * (NT * b + t + 1), bias_loaded, 32)
                nc.gpsimd.tensor_scalar(resid[:, t, :], resid[:, t, :], neg_mean[:, t, :], rstd[:, t, :], ALU.add, ALU.mult).then_inc(y_ready, 1)

            pool.wait_ge(mask_ready, A)
            pool.wait_ge(bias_loaded, 32)

            def body(b, first, last):
                if not first:
                    spread(b - 1, 2)
                    low_part(b - 1, 2)
                spread(b, 0)
                if not first:
                    for t in range(NT):
                        normalise(b - 1, t)
                spread(b, 1)
                low_part(b, 0)
                add_bias(b)
                low_part(b, 1)

            def last_part():
                spread(B - 1, 2)
                for t in range(NT):
                    normalise(B - 1, t)

            bodies(pool, body, last_part)

        @block.tensor
        def _(pe):
            def turn_w(i, bank):
                w, t = divmod(i, G)
                pe.wait_ge(w_loaded[w], 16)
                for s in range(G):
                    last = pe.transpose(bank[:, s * P:(s + 1) * P], w_rows[:, w, s, t * P:(t + 1) * P], ident[:, :])
                last.then_inc(w_turned, 1)

            def turn_x(b, t, bank):
                pe.wait_ge(x_loaded, 16 * (b + 1))
                for s in range(NT):
                    last = pe.transpose(bank[:, s * P:(s + 1) * P], x_rows[:, s, t * P:(t + 1) * P], ident[:, :])
                last.then_inc(x_turned, 1)

            def three_products(dst, pairs, done, piece):
                for n, (lhs, rhs) in enumerate(pairs):
                    if piece in (None, n * G // len(pairs)):
                        last = pe.matmul(dst, lhs, rhs, start=(n == 0), stop=(n == len(pairs) - 1))
                if piece in (None, G - 1):
                    last.then_inc(done, 1)

            def parts(left, left_cols, right, right_cols):
                return [(left[i][:, t, left_cols], right[j][:, t, right_cols])
                        for t in range(G) for i, j in ((0, 0), (0, 1), (1, 0))]

            def weight(w):
                return (w_hi[:, w], w_lo[:, w])

            def project_kq(b, w, g, bank, piece):
                pe.wait_ge(x_lo_ready, G * (b + 1))
                three_products(bank[:, :], parts(weight(w), slice(g * P, (g + 1) * P), (xt_hi, xt_lo), slice(0, N)), kq_done, piece)

            def linear_sums(b, g, bank):
                pe.wait_ge(k_sum_ready, G * b + g + 1)
                pe.wait_ge(kq_hi_ready, 2 * G * b + 2 * g + 2)
                for t in range(NT):
                    rows = slice(t * P, (t + 1) * P)
                    last = pe.matmul(bank[:, rows], qt_hi[:, g, rows], k_sum_heads[:, :], start=True, stop=True)
                last.then_inc(lin_done, 1)

            def project_v(b, t, bank, piece):
                three_products(bank[:, 0:D], parts((xt_hi, xt_lo), slice(t * P, (t + 1) * P), weight(2), slice(0, D)), v_done, piece)

            def project_out(b, t, bank, piece):
                pe.wait_ge(o_lo_ready, G * b + (G if piece is None else piece + 1))
                three_products(bank[:, 0:D], parts((ot_hi, ot_lo), slice(t * P, (t + 1) * P), weight(3), slice(0, D)), proj_done, piece)

            def turn_recip(b, g, bank):
                pe.wait_ge(recip_ready, G * b + g + 1)
                for t in range(NT):
                    last = pe.transpose(bank[:, t * P:(t + 1) * P], recip_heads[:, t * A:(t + 1) * A, :].rearrange("p a d -> p (a d)"), ident[:, :])
                last.then_inc(r_done, 1)

            def scores(b, u):
                g, half, a, n2, t = unit(u)
                if half == 0 and n2 == 0:
                    pe.wait_ge(stack_loaded[g][a], 16 * STACK_DMAS * (b + 1))
                wait(pe, max_done, UNITS * b + u + 1 - SCORE_BANKS)
                pe.matmul(score_bank[u % SCORE_BANKS][:, :], q_stack[:, g, a, t * P:(t + 1) * P], k_stack[:, g, a, :],
                          start=True, stop=True).then_inc(scores_done, 1)

            def turn_p(b, u):
                pe.wait_ge(exp_done, UNITS * b + u + 1)
                if ((u - 2) % UNITS) in (vector_units(b) if u >= 2 else VECTOR_UNITS):
                    wait(pe, pt_by_vector, vector_evacs(b, u - 2))
                else:
                    wait(pe, pt_by_scalar, scalar_evacs(b, u - 2))
                for m in range(NT):
                    last = pe.transpose(turn_bank[u % 2][:, m * P:(m + 1) * P], p_rows[:, u % SLOTS, m * P:(m + 1) * P], ident[:, :])
                last.then_inc(turned, 1)

            def weigh_v(b, h, m):
                g, half = divmod(h, HALVES)
                if h == 0:
                    pe.wait_ge(v_ready, NT * b + m + 1)
                if m == 0:
                    if half == 0:
                        wait(pe, o_ready, G * b + g)
                    pe.wait_ge(pt_by_vector, vector_evacs(b, UNITS_H * (h + 1) - 1))
                    pe.wait_ge(pt_by_scalar, scalar_evacs(b, UNITS_H * (h + 1) - 1))
                for a in range(A):
                    head = g * P + a * HD
                    last = pe.matmul(o_bank[a * HD:(a + 1) * HD, half * HN:(half + 1) * HN], v_rows[:, m, head:head + HD],
                                     pt_tile(h)[:, a, m, :], start=(m == 0), stop=(m == NT - 1), tile_position=(0, a * HD))
                if m == NT - 1:
                    last.then_inc(pv_done, 1)

            def chunk(b, kind, index, bank, piece=None):
                if kind == "w":
                    turn_w(index, bank)
                if kind == "x":
                    turn_x(b, index, bank)
                if kind in ("k", "q"):
                    project_kq(b, int(kind == "q"), index, bank, piece)
                if kind == "lin":
                    linear_sums(b, index, bank)
                if kind == "v":
                    project_v(b, index, bank, piece)
                if kind == "o":
                    project_out(b, index, bank, piece)
                if kind == "r":
                    turn_recip(b, index, bank)

            def bank_free(chunk):
                if chunk is not None:
                    kind, index, b = chunk
                    pe.wait_ge(*{
                        "w": (w_lo_ready, index + 1),
                        "x": (x_lo_ready, G * b + index + 1),
                        "k": (kq_lo_ready, 2 * G * b + 2 * index + 1),
                        "q": (kq_lo_ready, 2 * G * b + 2 * index + 2),
                        "lin": (lin_read, G * b + index + 1),
                        "v": (v_ready, NT * b + index + 1),
                        "o": (norm_step, 3 * (NT * b + index) + 1),
                        "r": (r_ready, G * b + index + 1),
                    }[kind])

            pe.wait_ge(ident_ready, 1)
            for i, (kind, index, bank) in enumerate(FIRST_CHUNKS):
                bank_free(before_in_list(FIRST_CHUNKS, i, bank, 0))
                if kind == "k" and index == 0:
                    pe.wait_ge(w_lo_ready, 2 * G)
                chunk(0, kind, index, first_banks[bank])
            for u in range(SCORES_AHEAD):
                scores(0, u)
            pe.wait_ge(w_lo_ready, 4 * G)

            def body(b, first, last):
                for s in range(UNITS):
                    u, rel = ahead(s, SCORES_AHEAD, last)
                    if u is not None:
                        scores(b + rel, u)
                    for h, m, rel in pv_pieces(s, first):
                        weigh_v(b + rel, h, m)
                    turn_p(b, s)
                    for i, (steps, kind, index, rel, bank) in enumerate(chunks_of(first, last)):
                        if s in steps:
                            if s == steps[0]:
                                bank_free(before_in_bank(bank, i, b, first, last))
                            for piece, at in enumerate(steps):
                                if at == s:
                                    chunk(b + rel, kind, index, chunk_banks[bank], piece if len(steps) > 1 else None)

            def last_part():
                for m in range(NT):
                    weigh_v(B - 1, NHALF - 1, m)
                bank_free(before_in_bank(1, len(LAST_BODY), B - 1, False, True))
                chunk(B - 1, "r", 2, chunk_banks[1])
                pe.wait_ge(max_done, UNITS * B)
                bank_free(before_in_bank(0, len(LAST_BODY), B - 1, False, True))
                for piece in range(G - 1):
                    for t in range(NT):
                        chunk(B - 1, "o", t, last_banks[t], piece)
                for t in range(NT):
                    chunk(B - 1, "o", t, last_banks[t], G - 1)

            bodies(pe, body, last_part)

        @block.scalar
        def _(act):
            def exponential(b, u):
                act.wait_ge(max_done, UNITS * b + u + 1)
                nc.scalar.activation(p_rows[:, u % SLOTS, :], p_rows[:, u % SLOTS, :], ACT.Exp, bias=neg_max[:, u:u + 1],
                                     scale=-1.0, accum_out=row_sum[:, u:u + 1]).then_inc(exp_done, 1)

            def chunk(b, kind, index, bank):
                if kind == "w":
                    w, t = divmod(index, G)
                    act.wait_ge(w_turned, index + 1)
                    nc.scalar.activation(w_hi[:, w, t, :], bank[:, 0:D], ACT.Copy, scale=SCALE if w == 1 else 1.0).then_inc(w_hi_ready, 1)
                if kind == "x":
                    act.wait_ge(x_turned, G * b + index + 1)
                    nc.scalar.activation(xt_hi[:, index, :], bank[:, :], ACT.Copy).then_inc(x_hi_ready, 1)
                if kind in ("k", "q"):
                    act.wait_ge(kq_done, 2 * G * b + 2 * index + 1 + (kind == "q"))
                    if kind == "k":
                        for a in range(A):
                            wait(act, stack_loaded[index][a], 16 * STACK_DMAS * b)
                        nc.scalar.activation(kt_hi[:, index, :], bank[:, :], ACT.Copy, accum_out=k_sum[:, index:index + 1]).then_inc(kq_hi_ready, 1)
                    else:
                        nc.scalar.activation(qt_hi[:, index, :], bank[:, :], ACT.Copy).then_inc(kq_hi_ready, 1)
                if kind == "r":
                    act.wait_ge(r_done, G * b + index + 1)
                    wait(act, o_lo_ready, G * b + index)
                    nc.scalar.activation(o_cols[:, :], bank[:, :], ACT.Copy).then_inc(r_ready, 1)

            def round_o(b, g):
                act.wait_ge(o_ready, G * b + g + 1)
                if g == 0:
                    wait(act, proj_done, NT * b)
                nc.scalar.activation(ot_hi[:, g, :], o_cols[:, :], ACT.Copy).then_inc(o_hi_ready, 1)

            def take_pt(b, u):
                g, half, a, n2, t = unit(u)
                h = g * HALVES + half
                act.wait_ge(turned, UNITS * b + u + 1)
                wait(act, pv_done, NHALF * b + h - 1)
                nc.scalar.activation(pt_tile(h)[:, a, :, n2 * P:(n2 + 1) * P],
                                     turn_bank[u % 2][:, :].rearrange("p (m n) -> p m n", m=NT), ACT.Copy).then_inc(pt_by_scalar, 1)

            def store(b, t):
                act.wait_ge(y_ready, NT * b + t + 1)
                act.dma_start(out[bass.ds(b, 1), t * P:(t + 1) * P, :].rearrange("o p d -> p (o d)"), resid[:, t, :]).then_inc(stored, 16)

            def load_x(b):
                wait(act, x_turned, G * b)
                act.dma_start(x_rows[:, :, :], x[bass.ds(b, 1)].rearrange("o (t p) d -> p (o t) d", p=P)).then_inc(x_loaded, 16)

            load_x(0)
            for kind, index, bank in FIRST_CHUNKS:
                chunk(0, kind, index, first_banks[bank])
            for u in range(AHEAD):
                exponential(0, u)

            def body(b, first, last):
                for s in range(UNITS):
                    if s not in vector_units(b):
                        take_pt(b, s)
                    u, rel = ahead(s, AHEAD, last)
                    if u is not None:
                        exponential(b + rel, u)
                    if s == LOAD_X_STEP and not last:
                        load_x(b + 1)
                    for kind, index, rel, bank in done_chunks(s, first, last):
                        chunk(b + rel, kind, index, bank)
                    if s in ROUND_STEP and not (first and s == ROUND_STEP[2]):
                        g = ROUND_STEP.index(s)
                        round_o(b - (g == 2), g)
                    if s in STORE_STEP and not first:
                        store(b - 1, STORE_STEP.index(s))

            def last_part():
                chunk(B - 1, "r", 2, chunk_banks[1])
                round_o(B - 1, 2)
                for t in range(NT):
                    store(B - 1, t)

            bodies(act, body, last_part)

        @block.vector
        def _(dve):
            def row_max(b, u):
                g, half, a, n2, t = unit(u)
                if u in (0, 1, UNITS_H, UNITS_H + 1):
                    dve.wait_ge(adj_loaded[t], 16 * (b + 1))
                wait(dve, turned, UNITS * b + u + 1 - SLOTS)
                wait_apart(dve, scores_done, UNITS * b + u + 1, adj_loaded[t], 16)
                nc.vector.tensor_tensor_reduce(p_rows[:, u % SLOTS, :], score_bank[u % SCORE_BANKS][:, :], adj_rows[:, t, :], -1.0, BIG,
                                               ALU.add, ALU.min, neg_max[:, u:u + 1]).then_inc(max_done, 1)

            def chunk(b, kind, index, bank):
                if kind == "w":
                    w, t = divmod(index, G)
                    dve.wait_ge(w_hi_ready, index + 1)
                    nc.vector.scalar_tensor_tensor(w_lo[:, w, t, :], bank[:, 0:D], SCALE if w == 1 else 1.0,
                                                   w_hi[:, w, t, :].bitcast(F32), ALU.mult, ALU.subtract).then_inc(w_lo_ready, 1)
                if kind == "x":
                    dve.wait_ge(x_hi_ready, G * b + index + 1)
                    nc.vector.tensor_tensor(xt_lo[:, index, :], bank[:, :], xt_hi[:, index, :].bitcast(F32), ALU.subtract).then_inc(x_lo_ready, 1)
                if kind in ("k", "q"):
                    hi, lo = (kt_hi, kt_lo) if kind == "k" else (qt_hi, qt_lo)
                    dve.wait_ge(kq_hi_ready, 2 * G * b + 2 * index + 1 + (kind == "q"))
                    if kind == "k":
                        wait(dve, lin_done, G * b + index)
                        nc.vector.tensor_scalar(k_sum_heads[:, :], head_mask[:, :], k_sum[:, index:index + 1], None, ALU.mult).then_inc(k_sum_ready, 1)
                    nc.vector.tensor_tensor(lo[:, index, :], bank[:, :], hi[:, index, :].bitcast(F32), ALU.subtract).then_inc(kq_lo_ready, 1)
                if kind == "lin":
                    dve.wait_ge(lin_done, G * b + index + 1)
                    of_heads = bank[:, :].rearrange("p (h n a d) -> p h a n d", h=HALVES, n=PER_HALF, a=A)[:, :, :, :, 0]
                    nc.vector.tensor_copy(lin_next[:, index * UNITS_G:(index + 1) * UNITS_G].rearrange("p (h a n) -> p h a n", h=HALVES, a=A),
                                          of_heads).then_inc(lin_read, 1)
                if kind == "v":
                    dve.wait_ge(v_done, NT * b + index + 1)
                    nc.vector.tensor_tensor(v_rows[:, index, :], bank[:, 0:D], bv_rows[:, :], ALU.add).then_inc(v_ready, 1)
                if kind == "o":
                    residual_norm(b, index, bank)

            def residual_norm(b, t, bank):
                done = 3 * (NT * b + t)
                dve.wait_ge(proj_done, NT * b + t + 1)
                dve.wait_ge(resid_ready, b + 1)
                nc.vector.tensor_tensor(resid[:, t, :], bank[:, 0:D], resid[:, t, :], ALU.add).then_inc(norm_step, 1)
                dve.wait_ge(norm_step, done + 1)
                nc.vector.bn_stats(bn[:, t, :], resid[:, t, :]).then_inc(norm_step, 1)
                wait_apart(dve, norm_step, done + 2, norm_step, 1)
                nc.vector.bn_aggr(mv[:, t, :], bn[:, t, :]).then_inc(norm_step, 1)

            def sum_adj(b, half):
                wait(dve, recip_ready, G * b)
                nc.vector.tensor_reduce(adj_sum[:, half * PER_HALF:(half + 1) * PER_HALF],
                                        adj_rows[:, half * PER_HALF:(half + 1) * PER_HALF, :], AX.X, ALU.add).then_inc(adj_summed, 1)

            def move_lin(b):
                dve.wait_ge(lin_read, G * (b + 1))
                wait(dve, recip_ready, G * b)
                nc.vector.tensor_copy(lin[:, :], lin_next[:, :]).then_inc(lin_moved, 1)

            def reciprocals(b, g):
                dve.wait_ge(exp_done, UNITS * b + (g + 1) * UNITS_G)
                wait(dve, recip_ready, G * b + g)
                nc.vector.reciprocal(recip[:, :], row_sum[:, g * UNITS_G:(g + 1) * UNITS_G]).then_inc(recip_made, 1)

            def divide_o(b, g):
                dve.wait_ge(r_ready, G * b + g + 1)
                dve.wait_ge(pv_done, NHALF * b + (g + 1) * HALVES)
                nc.vector.tensor_tensor(o_cols[:, :], o_bank[:, :], o_cols[:, :], ALU.mult).then_inc(o_ready, 1)

            def take_pt(b, u):
                g, half, a, n2, t = unit(u)
                h = g * HALVES + half
                dve.wait_ge(turned, UNITS * b + u + 1)
                wait(dve, pv_done, NHALF * b + h - 1)
                nc.vector.tensor_copy(pt_tile(h)[:, a, :, n2 * P:(n2 + 1) * P],
                                      turn_bank[u % 2][:, :].rearrange("p (m n) -> p m n", m=NT)).then_inc(pt_by_vector, 1)

            dve.wait_ge(mask_ready, A)
            for kind, index, bank in FIRST_CHUNKS:
                chunk(0, kind, index, first_banks[bank])
            dve.wait_ge(bias_loaded, 32)
            for u in range(AHEAD):
                row_max(0, u)

            def body(b, first, last):
                for s in range(UNITS):
                    u, rel = ahead(s, AHEAD, last)
                    if u is not None:
                        row_max(b + rel, u)
                    if s == MOVE_LIN_STEP:
                        move_lin(b)
                    if s in ADJ_SUM_STEP:
                        sum_adj(b, ADJ_SUM_STEP.index(s))
                    if s in RECIP_STEP:
                        reciprocals(b, RECIP_STEP.index(s))
                    for kind, index, rel, bank in done_chunks(s - VECTOR_READS_AFTER, first, last):
                        chunk(b + rel, kind, index, bank)
                    if s in DIVIDE_STEP and not (first and s == DIVIDE_STEP[2]):
                        g = DIVIDE_STEP.index(s)
                        divide_o(b - (g == 2), g)
                    if s in vector_units(b):
                        take_pt(b, s)

            def last_part():
                divide_o(B - 1, 2)
                dve.wait_ge(o_hi_ready, G * B)
                nc.vector.tensor_tensor(ot_lo[:, G - 1, :], o_cols[:, :], ot_hi[:, G - 1, :].bitcast(F32), ALU.subtract).then_inc(o_lo_ready, 1)
                for t in range(NT):
                    residual_norm(B - 1, t, last_banks[t])

            bodies(dve, body, last_part)


OUTPUT = ((B, N, D), "float32")


def kernel(x, adj, L0_gnn_Wq, L0_gnn_Wk, L0_gnn_Wv, L0_gnn_bv, L0_gnn_Wo, L0_gnn_bo):
    import numpy as np
    import concourse.bacc as bacc
    from concourse.bass_utils import run_bass_kernel_spmd

    nc = bacc.Bacc("TRN2", target_bir_lowering=False, num_devices=1)
    given = {"x": x, "adj": adj, "wq": L0_gnn_Wq, "wk": L0_gnn_Wk, "wv": L0_gnn_Wv, "bv": L0_gnn_bv,
             "wo": L0_gnn_Wo, "bo": L0_gnn_bo}
    arrays = {name: np.ascontiguousarray(a) for name, a in given.items()}
    args = [nc.dram_tensor(name, a.shape, mybir.dt.from_np(a.dtype), kind="ExternalInput").ap() for name, a in arrays.items()]
    shape, dtype = OUTPUT
    out = nc.dram_tensor("out", shape, mybir.dt.from_np(np.dtype(dtype)), kind="ExternalOutput").ap()
    build(nc, *args, out)
    return run_bass_kernel_spmd(nc, [arrays], core_ids=[0]).results[0]["out"]
```
